# Optimizing a Trainium2 kernel written in Bass

```python
import numpy as np
import jax
import jax.numpy as jnp

def _softmax(x, axis=-1):
    return jax.nn.softmax(x, axis=axis)

def _gelu(x):
    return jax.nn.gelu(x, approximate=True)

def _silu(x):
    return jax.nn.silu(x)

def _sigmoid(x):
    return jax.nn.sigmoid(x)

def _layernorm(x, axis=-1, eps=1e-05):
    m = jnp.mean(x, axis=axis, keepdims=True)
    v = jnp.var(x, axis=axis, keepdims=True)
    return (x - m) / jnp.sqrt(v + eps)

def _scatter_add(tgt, idx, src, axis=0):
    return tgt.at[idx].add(src)

def _segment_sum(src, seg, n):
    return jax.ops.segment_sum(src, seg, n)
kernel_name = 'mk_xattn_ffn_d1_seqx_r4_487257'

def setup_inputs(seed: int=0):
    np.random.seed(seed)
    _w = jnp.asarray

    def _rec_inputs():
        import jax
        import jax.numpy as jnp
        _rk = jax.random.key(seed)
        x = 4.136e-05 + 0.9999 * jax.random.normal(jax.random.fold_in(_rk, 1), (4, 512, 512), jnp.float32)
        _lenS = 512 - jax.random.randint(jax.random.fold_in(_rk, 7), (4,), 0, max(1, 512 // 4) + 1, jnp.int32)
        _lenS2 = 512 - jax.random.randint(jax.random.fold_in(_rk, 8), (4,), 0, max(1, 512 // 4) + 1, jnp.int32)
        _ctx_1024P = jax.random.normal(jax.random.fold_in(_rk, 11), (4, 16, 256), jnp.float32)
        _ctx_1024c = jax.random.dirichlet(jax.random.fold_in(_rk, 511), 0.3 * jnp.ones((16,), jnp.float32), (4, 512))
        _ctx_1024t = jnp.einsum('bsk,bkd->bsd', _ctx_1024c, _ctx_1024P)
        _ctx_1024t = _ctx_1024t * jax.lax.rsqrt(jnp.mean(jnp.square(_ctx_1024t)) + 1e-12) * 0.953939
        ctx_1024 = -0.000292821 + 1.00034 * (_ctx_1024t + 0.3 * jax.random.normal(jax.random.fold_in(_rk, 611), (4, 512, 256), jnp.float32))
        return (x, ctx_1024)
    x, ctx_1024 = _rec_inputs()

    def _L0_xattn_setup():
        import jax, jax.numpy as jnp
        import numpy as np
        import math
        B, L, DM = (2, 512, 256)
        DS, DC, EXP = (16, 4, 2)
        DI = EXP * DM
        DR = math.ceil(DM / 16)
        DT_MIN, DT_MAX, DT_FLOOR = (0.001, 0.1, 0.0001)

        def _ssm_forward(hidden_states, z, in_proj_w, conv_w, conv_b, x_proj_w, dt_proj_w, dt_proj_b, A_log, D):
            b = hidden_states.shape[0]
            x = jnp.einsum('ed,bld->bel', in_proj_w, hidden_states)
            xp = jnp.pad(x, ((0, 0), (0, 0), (DC - 1, 0)))
            xc = jax.lax.conv_general_dilated(xp, conv_w[:, None, :], window_strides=(1,), padding='VALID', dimension_numbers=('NCH', 'OIH', 'NCH'), feature_group_count=DI)
            u = jax.nn.silu(xc + conv_b[None, :, None])
            x_dbl = jnp.einsum('ke,bel->bkl', x_proj_w, u)
            dt_lo = x_dbl[:, :DR]
            Bm = x_dbl[:, DR:DR + DS]
            Cm = x_dbl[:, DR + DS:]
            delta = jax.nn.softplus(jnp.einsum('er,brl->bel', dt_proj_w, dt_lo) + dt_proj_b[None, :, None])
            A = -jnp.exp(A_log)

            def step(state, xs):
                d_t, B_t, C_t, u_t = xs
                dA = jnp.exp(d_t[..., None] * A)
                state = state * dA + (d_t * u_t)[..., None] * B_t[:, None, :]
                y_t = jnp.einsum('ben,bn->be', state, C_t)
                return (state, y_t)
            xs = (jnp.moveaxis(delta, -1, 0), jnp.moveaxis(Bm, -1, 0), jnp.moveaxis(Cm, -1, 0), jnp.moveaxis(u, -1, 0))
            state0 = jnp.zeros((b, DI, DS), delta.dtype)
            _, ys = jax.lax.scan(step, state0, xs)
            y = jnp.moveaxis(ys, 0, -1)
            y = y + D[None, :, None] * u
            y = y * jax.nn.silu(z)
            return jnp.swapaxes(y, 1, 2)
        key = jax.random.key(seed)
        ks = jax.random.split(key, 8)
        hidden_states = jax.random.normal(ks[0], (B, L, DM), jnp.float32)
        z = jax.random.normal(ks[1], (B, DI, L), jnp.float32)
        in_proj_w = jax.random.normal(ks[2], (DI, DM), jnp.float32) * DM ** (-0.5)
        conv_w = jax.random.normal(ks[3], (DI, DC), jnp.float32) * DC ** (-0.5)
        conv_b = jnp.zeros((DI,), jnp.float32)
        x_proj_w = jax.random.normal(ks[4], (DR + 2 * DS, DI), jnp.float32) * DI ** (-0.5)
        dt_std = DR ** (-0.5)
        dt_proj_w = jax.random.uniform(ks[5], (DI, DR), jnp.float32, -dt_std, dt_std)
        dt = jnp.exp(jax.random.uniform(ks[6], (DI,), jnp.float32) * (math.log(DT_MAX) - math.log(DT_MIN)) + math.log(DT_MIN))
        dt = jnp.clip(dt, DT_FLOOR)
        dt_proj_b = dt + jnp.log(-jnp.expm1(-dt))
        A_log = jnp.log(jnp.broadcast_to(jnp.arange(1, DS + 1, dtype=jnp.float32), (DI, DS)))
        D = jnp.ones((DI,), jnp.float32)
        return dict(hidden_states=hidden_states, z=z, in_proj_w=in_proj_w, conv_w=conv_w, conv_b=conv_b, x_proj_w=x_proj_w, dt_proj_w=dt_proj_w, dt_proj_b=dt_proj_b, A_log=A_log, D=D)
    _L0_xattn_all = _L0_xattn_setup()
    _L0_xattn_in = {k: v for k, v in _L0_xattn_all.items() if k in ('in_proj_w', 'conv_w', 'conv_b', 'x_proj_w', 'dt_proj_w', 'dt_proj_b', 'A_log', 'D')}
    del _L0_xattn_all

    def _L0_ffn_setup():
        import jax, jax.numpy as jnp
        import numpy as np
        H = 512
        I = 352
        E = 16
        G = 4
        TOPK_GROUP = 2
        K = 4
        SI = 2 * I
        SCALE = 1.0
        NORM = True
        B, S = (4, 128)

        def _swiglu(h):
            g, u = jnp.split(h, 2, axis=-1)
            return jax.nn.silu(g) * u

        def _combine_weights(xt, gate_w):
            T = xt.shape[0]
            scores = jax.nn.softmax(xt @ gate_w.T, axis=-1)
            group_scores = scores.reshape(T, G, E // G).max(axis=-1)
            _, gidx = jax.lax.top_k(group_scores, TOPK_GROUP)
            gmask = jnp.zeros((T, G), bool).at[jnp.arange(T)[:, None], gidx].set(True)
            emask = jnp.repeat(gmask, E // G, axis=1)
            masked = jnp.where(emask, scores, 0.0)
            w, eidx = jax.lax.top_k(masked, K)
            if NORM:
                w = w / (w.sum(-1, keepdims=True) + 1e-20)
            w = w * SCALE
            return jnp.zeros((T, E), xt.dtype).at[jnp.arange(T)[:, None], eidx].add(w)
        key = jax.random.key(seed)
        ks = jax.random.split(key, 6)
        sc = lambda fan_in: 1.0 / np.sqrt(fan_in)
        return {'x': jax.random.normal(ks[0], (B, S, H), jnp.float32), 'gate_w': jax.random.normal(ks[1], (E, H), jnp.float32) * sc(H), 'expert_up_w': jax.random.normal(ks[2], (E, 2 * I, H), jnp.float32) * sc(H), 'expert_down_w': jax.random.normal(ks[3], (E, H, I), jnp.float32) * sc(I), 'shared_up_w': jax.random.normal(ks[4], (2 * SI, H), jnp.float32) * sc(H), 'shared_down_w': jax.random.normal(ks[5], (H, SI), jnp.float32) * sc(SI)}
    _L0_ffn_all = _L0_ffn_setup()
    _L0_ffn_in = {k: v for k, v in _L0_ffn_all.items() if k in ('gate_w', 'expert_up_w', 'expert_down_w', 'shared_up_w', 'shared_down_w')}
    del _L0_ffn_all
    return {'x': x, 'ctx_1024': ctx_1024, 'L0_xattn_in_proj_w': _L0_xattn_in['in_proj_w'], 'L0_xattn_conv_w': _L0_xattn_in['conv_w'], 'L0_xattn_conv_b': _L0_xattn_in['conv_b'], 'L0_xattn_x_proj_w': _L0_xattn_in['x_proj_w'], 'L0_xattn_dt_proj_w': _L0_xattn_in['dt_proj_w'], 'L0_xattn_dt_proj_b': _L0_xattn_in['dt_proj_b'], 'L0_xattn_A_log': _L0_xattn_in['A_log'], 'L0_xattn_D': _L0_xattn_in['D'], 'L0_ffn_gate_w': _L0_ffn_in['gate_w'], 'L0_ffn_expert_up_w': _L0_ffn_in['expert_up_w'], 'L0_ffn_expert_down_w': _L0_ffn_in['expert_down_w'], 'L0_ffn_shared_up_w': _L0_ffn_in['shared_up_w'], 'L0_ffn_shared_down_w': _L0_ffn_in['shared_down_w']}

def reference(x, ctx_1024, L0_xattn_in_proj_w, L0_xattn_conv_w, L0_xattn_conv_b, L0_xattn_x_proj_w, L0_xattn_dt_proj_w, L0_xattn_dt_proj_b, L0_xattn_A_log, L0_xattn_D, L0_ffn_gate_w, L0_ffn_expert_up_w, L0_ffn_expert_down_w, L0_ffn_shared_up_w, L0_ffn_shared_down_w):
    import jax
    import jax.numpy as jnp

    def _L0_xattn_ref(hidden_states, z, in_proj_w, conv_w, conv_b, x_proj_w, dt_proj_w, dt_proj_b, A_log, D):
        import jax, jax.numpy as jnp
        import numpy as np
        import math
        B, L, DM = (2, 512, 256)
        DS, DC, EXP = (16, 4, 2)
        DI = EXP * DM
        DR = math.ceil(DM / 16)
        DT_MIN, DT_MAX, DT_FLOOR = (0.001, 0.1, 0.0001)

        def _ssm_forward(hidden_states, z, in_proj_w, conv_w, conv_b, x_proj_w, dt_proj_w, dt_proj_b, A_log, D):
            b = hidden_states.shape[0]
            x = jnp.einsum('ed,bld->bel', in_proj_w, hidden_states)
            xp = jnp.pad(x, ((0, 0), (0, 0), (DC - 1, 0)))
            xc = jax.lax.conv_general_dilated(xp, conv_w[:, None, :], window_strides=(1,), padding='VALID', dimension_numbers=('NCH', 'OIH', 'NCH'), feature_group_count=DI)
            u = jax.nn.silu(xc + conv_b[None, :, None])
            x_dbl = jnp.einsum('ke,bel->bkl', x_proj_w, u)
            dt_lo = x_dbl[:, :DR]
            Bm = x_dbl[:, DR:DR + DS]
            Cm = x_dbl[:, DR + DS:]
            delta = jax.nn.softplus(jnp.einsum('er,brl->bel', dt_proj_w, dt_lo) + dt_proj_b[None, :, None])
            A = -jnp.exp(A_log)

            def step(state, xs):
                d_t, B_t, C_t, u_t = xs
                dA = jnp.exp(d_t[..., None] * A)
                state = state * dA + (d_t * u_t)[..., None] * B_t[:, None, :]
                y_t = jnp.einsum('ben,bn->be', state, C_t)
                return (state, y_t)
            xs = (jnp.moveaxis(delta, -1, 0), jnp.moveaxis(Bm, -1, 0), jnp.moveaxis(Cm, -1, 0), jnp.moveaxis(u, -1, 0))
            state0 = jnp.zeros((b, DI, DS), delta.dtype)
            _, ys = jax.lax.scan(step, state0, xs)
            y = jnp.moveaxis(ys, 0, -1)
            y = y + D[None, :, None] * u
            y = y * jax.nn.silu(z)
            return jnp.swapaxes(y, 1, 2)
        return _ssm_forward(hidden_states, z, in_proj_w, conv_w, conv_b, x_proj_w, dt_proj_w, dt_proj_b, A_log, D)

    def _L0_ffn_ref(x, gate_w, expert_up_w, expert_down_w, shared_up_w, shared_down_w):
        import jax, jax.numpy as jnp
        import numpy as np
        H = 512
        I = 352
        E = 16
        G = 4
        TOPK_GROUP = 2
        K = 4
        SI = 2 * I
        SCALE = 1.0
        NORM = True
        B, S = (4, 128)

        def _swiglu(h):
            g, u = jnp.split(h, 2, axis=-1)
            return jax.nn.silu(g) * u

        def _combine_weights(xt, gate_w):
            T = xt.shape[0]
            scores = jax.nn.softmax(xt @ gate_w.T, axis=-1)
            group_scores = scores.reshape(T, G, E // G).max(axis=-1)
            _, gidx = jax.lax.top_k(group_scores, TOPK_GROUP)
            gmask = jnp.zeros((T, G), bool).at[jnp.arange(T)[:, None], gidx].set(True)
            emask = jnp.repeat(gmask, E // G, axis=1)
            masked = jnp.where(emask, scores, 0.0)
            w, eidx = jax.lax.top_k(masked, K)
            if NORM:
                w = w / (w.sum(-1, keepdims=True) + 1e-20)
            w = w * SCALE
            return jnp.zeros((T, E), xt.dtype).at[jnp.arange(T)[:, None], eidx].add(w)
        Bq, Sq, _ = x.shape
        xt = x.reshape(-1, H)
        cw = _combine_weights(xt, gate_w)
        out = jnp.zeros_like(xt)
        for e in range(E):
            a = _swiglu(xt @ expert_up_w[e].T)
            out = out + cw[:, e:e + 1] * (a @ expert_down_w[e].T)
        out = out + _swiglu(xt @ shared_up_w.T) @ shared_down_w.T
        return out.reshape(Bq, Sq, H)
    x = x + _L0_xattn_ref(ctx_1024, _layernorm(x, axis=-1), L0_xattn_in_proj_w, L0_xattn_conv_w, L0_xattn_conv_b, L0_xattn_x_proj_w, L0_xattn_dt_proj_w, L0_xattn_dt_proj_b, L0_xattn_A_log, L0_xattn_D)
    x = x + _L0_ffn_ref(_layernorm(x, axis=-1), L0_ffn_gate_w, L0_ffn_expert_up_w, L0_ffn_expert_down_w, L0_ffn_shared_up_w, L0_ffn_shared_down_w)
    return x

_drawn_inputs = setup_inputs


def setup_inputs(seed=0):
    import zlib

    import numpy as np

    out = dict(_drawn_inputs(seed))
    spreads = {'L0_xattn_conv_b': (0.0, 0.1), 'L0_xattn_D': (1.0, 0.2)}
    factors = {}
    for name, (base, spread) in spreads.items():
        noise = np.random.default_rng([zlib.crc32(name.encode()), seed]).standard_normal(out[name].shape)
        drawn = base * np.exp(spread * noise) if base else spread * noise
        out[name] = jnp.asarray(drawn.astype(out[name].dtype))
    for name, factor in factors.items():
        out[name] = (out[name] * factor).astype(out[name].dtype)
    return out
```

```python
from contextlib import ExitStack

import concourse.bass as bass
from concourse import mybir

F32 = mybir.dt.float32
F16 = mybir.dt.float16
BF16 = mybir.dt.bfloat16
U32 = mybir.dt.uint32
I32 = mybir.dt.int32
ALU = mybir.AluOpType
ACT = mybir.ActivationFunctionType
AX = mybir.AxisListType

P = 128
NB = 4
L = 512
DM = 256
H = 512
DS = 16
DR = 16
TAPS = 4
ET = H // P
LC = L // P
T = NB * L
NT = T // P
E = 16
G = 4
EPS = 1e-5
SG = DS // 4
KT = H // P
I = 352
TOPK = 4
NS = 2
TB = 256
BT = TB // P
NSB = NS * T // TB
NRB = (T * TOPK + E * (TB - 1)) // TB
NBLK = NSB + NRB
MAXB = T // TB
RW = 2 * H + 4
WS = 64.0
IC = [(c * P, min(P, I - c * P)) for c in range(-(-I // P))]
NC = len(IC)


def build(nc, x, ctxT, in_projT, conv_w, conv_b, x_projT, dt_projT, dt_b, A_log, D, gateT, upT, downA, downB, out):
    bc_dram = nc.dram_tensor("bc_dram", (NB, 2 * DS, L), F32, kind="Internal").ap()
    rows_dram = nc.dram_tensor("rows_dram", (T, RW // 2), U32, kind="Internal").ap()
    slots_dram = nc.dram_tensor("slots_dram", (NRB * TB, RW // 2), U32, kind="Internal").ap()

    with ExitStack() as ctx:
        def sb(name, shape, dt=F32):
            return ctx.enter_context(nc.sbuf_tensor(name, shape, dt))

        def pb(name):
            return ctx.enter_context(nc.psum_tensor(name, [P, 512], F32))

        def sem(name):
            return ctx.enter_context(nc.semaphore(name))

        ident = sb("ident", [P, P])
        inp_w = sb("inp_w", [P, DM // P, H])
        xp_w = sb("xp_w", [P, ET, DR + 2 * DS])
        dt_w = sb("dt_w", [DR, H])
        taps = sb("taps", [P, ET, TAPS])
        taps_half = sb("taps_half", [P, ET, TAPS])
        cbias = sb("cbias", [P, ET])
        dtbias = sb("dtbias", [P, ET])
        alog = sb("alog", [P, ET * DS])
        negA = sb("negA", [P, ET * DS])
        Dcol = sb("Dcol", [P, ET])
        Ddiag = sb("Ddiag", [P, ET, P])
        gate_w = sb("gate_w", [P, H // P, E])
        powexp = sb("powexp", [P, 4])
        logits = sb("logits", [P, NT, E])
        wshared = sb("wshared", [P, 1])
        tokens = sb("tokens", [P, NT], I32)
        pad_row = sb("pad_row", [P, RW], F16)

        scan_mem = ExitStack()

        def sb(name, shape, dt=F32):
            return scan_mem.enter_context(nc.sbuf_tensor(name, shape, dt))

        def pb(name):
            return scan_mem.enter_context(nc.psum_tensor(name, [P, 512], F32))

        Bb = sb("Bb", [P, DS, L])
        Cb = sb("Cb", [P, DS, L])
        Cf = Cb[:].rearrange("p n l -> p (n l)")
        dBu = sb("dBu", [P, 2, 2, L])
        hc = sb("hc", [P, 4, L])
        delta = sb("delta", [P, 2, ET, L])
        u = sb("u", [P, 2, ET, L])
        du = sb("du", [P, 2, ET, L])
        xs = sb("xs", [P, 2, LC, H])
        ctxs = sb("ctxs", [P, DM // P, L])
        sz = sb("sz", [P, 2, ET, L])
        xin = sb("xin", [P, 2, L + TAPS - 1])
        cv = sb("cv", [P, 2, L])
        th = sb("th", [P, 2, L])
        xdbl = sb("xdbl", [DR + 2 * DS, L])
        yv = sb("yv", [P, ET, L])
        xn = sb("xn", [P, 2, H])
        xnT = th
        row = sb("row", [P, 2, RW], F16)
        stat = sb("stat", [P, 4, 6])
        mv = sb("mv", [P, 4, 2])
        veps = sb("veps", [P, 4])
        rstd = sb("rstd", [P, 4])
        nmr = sb("nmr", [P, 4])

        dA = [pb(f"dA{i}") for i in range(2)]
        yp = pb("yp")
        pp = [pb(f"pp{i}") for i in range(2)]
        pq = pb("pq")
        scan_mem.close()

        def sb(name, shape, dt=F32):
            return ctx.enter_context(nc.sbuf_tensor(name, shape, dt))

        ident16 = sb("ident16", [P, P], F16)
        up_raw = sb("up_raw", [P, 2, KT, 2 * I])
        dn_raw = sb("dn_raw", [P, 2, NC, H])
        up_hl = sb("up_hl", [P, 2, 2, KT, 2 * I], F16)
        dn_hl = sb("dn_hl", [P, 2, 2, NC, H], F16)
        xb = sb("xb", [P, 2, BT, RW], F16)
        xT = sb("xT", [P, 2, 2 * KT, TB], F16)
        sg = sb("sg", [P, NC, TB])
        a32 = sb("a32", [P, NC, TB])
        a_hl = sb("a_hl", [P, 2, 2, NC, TB], F16)
        yb = sb("yb", [P, 2, BT, H])
        meta = sb("meta", [P, NBLK * BT, 2], U32)
        dest = sb("dest", [P, 2, BT], U32)
        xr = sb("xr", [P, NT, RW], F16)
        r_max = sb("r_max", [P, NT])
        r_exp = sb("r_exp", [P, NT, E])
        r_sum = sb("r_sum", [P, NT])
        r_inv = sb("r_inv", [P, NT])
        score = sb("score", [P, NT, E])
        g_in = sb("g_in", [P, NT, 8])
        g_top = sb("g_top", [P, NT, 8])
        g_idx = sb("g_idx", [P, NT, 8], U32)
        g_idf = sb("g_idf", [P, NT, 8])
        g_mask = sb("g_mask", [P, NT, G])
        g_mask2 = sb("g_mask2", [P, NT, G])
        e_top = sb("e_top", [P, NT, 8])
        e_idx = sb("e_idx", [P, NT, 8], U32)
        e_idf = sb("e_idf", [P, NT, 8])
        w_top = sb("w_top", [P, NT, TOPK])
        onehot = sb("onehot", [P, TOPK, NT, E])
        picked = sb("picked", [P, NT, E])
        count = sb("count", [P, E, NT])
        cum_t = sb("cum_t", [P, E, NT])
        over = sb("over", [P, E, MAXB])
        nblk = sb("nblk", [P, E])
        cum_b = sb("cum_b", [P, E])
        base = sb("base", [P, E])
        place = sb("place", [P, NT, E])
        prod = sb("prod", [P, NT, E])
        slotf = sb("slotf", [P, TOPK, NT])
        slot = sb("slot", [P, TOPK, NT], U32)
        below = sb("below", [P, NRB, E])
        bexpf = sb("bexpf", [P, NRB])
        bexp = sb("bexp", [P, NRB], I32)
        iota_e = sb("iota_e", [P, E])
        iota_m = sb("iota_m", [P, MAXB])
        iota_b = sb("iota_b", [P, NRB])
        keep = sb("keep", [P, E, NT])
        ones = sb("ones", [P, P])
        before = sb("before", [P, P])

        def pb(name, shape=(P, 512), dt=F32):
            return ctx.enter_context(nc.psum_tensor(name, list(shape), dt))

        pt = [pb(f"pt{i}", (P, 2 * KT * P), F16) for i in range(BT)]
        pu = [pb(f"pu{i}") for i in range(NC)]
        py = [pb(f"py{i}") for i in range(BT)]

        w_in = sem("w_in")
        ctx_in = sem("ctx_in")
        x_in = sem("x_in")
        ident_ok = sem("ident_ok")
        pool_const = sem("pool_const")
        act_const = sem("act_const")
        dve_const = sem("dve_const")
        chain = sem("chain")
        inproj_done = sem("inproj_done")
        xin_ready = sem("xin_ready")
        conv_done = sem("conv_done")
        tanh_u = sem("tanh_u")
        u_ready = sem("u_ready")
        xproj_done = sem("xproj_done")
        xdbl_ready = sem("xdbl_ready")
        bc_stored = sem("bc_stored")
        b_ready = sem("b_ready")
        c_ready = sem("c_ready")
        dt_done = sem("dt_done")
        dt_read = sem("dt_read")
        dt_exp = sem("dt_exp")
        dt_log = sem("dt_log")
        delta_ready = sem("delta_ready")
        du_ready = sem("du_ready")
        ln_var = sem("ln_var")
        ln_rstd = sem("ln_rstd")
        ln_shift = sem("ln_shift")
        z_half = sem("z_half")
        tanh_z = sem("tanh_z")
        sz_ready = sem("sz_ready")
        dA_ready = sem("dA_ready")
        dbu_ready = sem("dbu_ready")
        scan_done = sem("scan_done")
        hc_ready = sem("hc_ready")
        sum_done = sem("sum_done")
        yv_done = sem("yv_done")
        yT_done = sem("yT_done")
        x2_ready = sem("x2_ready")
        xn_ready = sem("xn_ready")
        hi_ready = sem("hi_ready")
        row_ready = sem("row_ready")
        xnT_done = sem("xnT_done")
        xnT_copied = sem("xnT_copied")
        gate_done = sem("gate_done")
        lg_copied = sem("lg_copied")
        x2_stored = sem("x2_stored")
        row_stored = [sem(f"row_stored{i}") for i in range(2)]


        pad_ok = sem("pad_ok")
        pad_stored = sem("pad_stored")
        route_const = sem("route_const")
        shifted = sem("shifted")
        exp_ready = sem("exp_ready")
        mask_ready = sem("mask_ready")
        rank_done = sem("rank_done")
        experts_ready = sem("experts_ready")
        xr_in = sem("xr_in")
        xr_weight = sem("xr_weight")
        scattered = sem("scattered")
        up_in = [sem(f"up_in{i}") for i in range(2)]
        dn_in = [sem(f"dn_in{i}") for i in range(2)]
        rows_in = [sem(f"rows_in{i}") for i in range(2)]
        up_hi = sem("up_hi")
        up_lo = sem("up_lo")
        dn_hi = sem("dn_hi")
        dn_lo = sem("dn_lo")
        meta_ok = sem("meta_ok")
        xT_done = sem("xT_done")
        xT_copied = sem("xT_copied")
        up_done = sem("up_done")
        silu_ok = sem("silu_ok")
        a_ok = sem("a_ok")
        a_hi = sem("a_hi")
        a_lo = sem("a_lo")
        down_done = sem("down_done")
        y_ok = sem("y_ok")
        y_added = sem("y_added")
        add_turns = sem("add_turns")

        def wait(eng, s, v):
            if not isinstance(v, int) or v > 0:
                eng.wait_ge(s, v)

        def half_count(n, s, step):
            if isinstance(n, int):
                return step * (n // 2 + 1)
            return n * (step // 2) + (step - s * (step // 2))

        def expert_turns(eng, turn):
            turn(0, 0, True)
            turn(1, 1, True)
            with eng.Fori(1, (NBLK - 3) // 2) as i:
                turn(i * 2, 0, True)
                turn(i * 2 + 1, 1, True)
            for n in range((NBLK - 3) // 2 * 2, NBLK - 1):
                turn(n, n % 2, n + 2 < NBLK)

        block = ctx.enter_context(nc.Block())

        @block.sync
        def _(sp):
            for dst, src in ((inp_w[:], in_projT), (xp_w[:], x_projT), (dt_w[:], dt_projT), (taps[:], conv_w),
                             (cbias[:], conv_b), (dtbias[:], dt_b), (alog[:], A_log), (Dcol[:], D),
                             (gate_w[:], gateT)):
                sp.dma_start(dst, src).then_inc(w_in, 16)
            sp.wait_ge(pad_ok, 3)
            sp.dma_start(slots_dram.rearrange("(n p) c -> p n c", p=P),
                         pad_row[:].bitcast(U32).unsqueeze(1).to_broadcast([P, NRB * BT, RW // 2])).then_inc(pad_stored, 16)
            sp.dma_start(out[T:, :], pad_row[:, 0:2 * H].bitcast(F32)).then_inc(pad_stored, 16)
            for b in range(NB):
                sp.wait_ge(xdbl_ready, b + 1)
                sp.dma_start(bc_dram[b], xdbl[DR:, :]).then_inc(bc_stored, 16)
                sp.wait_ge(bc_stored, 16 * (b + 1))
                for q in range(SG):
                    if b:
                        sp.wait_ge(dbu_ready, 8 * (4 * b - 1) + 2 * q + 2)
                    sp.dma_start(Bb[:, 4 * q:4 * q + 4, :],
                                 bc_dram[b, 4 * q:4 * q + 4, :].partition_broadcast(P)).then_inc(b_ready, 16)
                    if b:
                        sp.wait_ge(hc_ready, 16 * (4 * b - 1) + 4 * q + 4)
                    sp.dma_start(Cb[:, 4 * q:4 * q + 4, :],
                                 bc_dram[b, DS + 4 * q:DS + 4 * q + 4, :].partition_broadcast(P)).then_inc(c_ready, 16)
                    sp.wait_ge(b_ready, 16 * (4 * b + q + 1))
                    sp.wait_ge(c_ready, 16 * (4 * b + q + 1))

            sp.wait_ge(row_ready, NT)
            sp.wait_ge(lg_copied, NT)
            for s in row_stored:
                sp.wait_ge(s, 16 * NT // 2)
            sp.wait_ge(x2_stored, 16 * NT)
            sp.dma_start(xr[:].bitcast(U32), rows_dram.rearrange("(t p) c -> p t c", p=P)).then_inc(xr_in, 16)

            def load_up(n, s, e):
                wait(sp, up_lo, n * KT - KT)
                sp.dma_start(up_raw[:, s], upT[bass.ds(e, 1)].squeeze(0)).then_inc(up_in[s], 16)

            def load_dn(n, s, e):
                wait(sp, dn_lo, n - 1)
                sp.dma_start(dn_raw[:, s, 0:2, :], downA[bass.ds(e, 1)].squeeze(0)).then_inc(dn_in[s], 16)
                sp.dma_start(dn_raw[0:IC[-1][1], s, 2, :], downB[bass.ds(e, 1)].squeeze(0)).then_inc(dn_in[s], 16)

            def load_rows(n, s, src):
                wait(sp, xT_done, n * BT - BT)
                wait(sp, meta_ok, n - 1)
                sp.dma_start(xb[:, s].bitcast(U32), src.rearrange("(t p) c -> p t c", p=P)).then_inc(rows_in[s], 16)

            half = NSB // NS
            for h in range(NS):
                def shared(i):
                    for s in range(2):
                        n = i * 2 + (h * half + s)
                        load_up(n, s, E + h)
                        load_dn(n, s, E + h)
                        load_rows(n, s, rows_dram[bass.ds(i * (2 * TB) + s * TB, TB), :])
                if h == 0:
                    shared(0)
                with sp.Fori(1 - h, half // 2) as i:
                    shared(i)
            sp.wait_ge(experts_ready, 1)

            def routed(i, s):
                n = i * 2 + (NSB + s)
                e = sp.value_load(bexp[0:1, bass.ds(i * 2 + s, 1)], min_val=0, max_val=E - 1)
                load_up(n, s, e)
                load_dn(n, s, e)
                load_rows(n, s, slots_dram[bass.ds(i * (2 * TB) + s * TB, TB), :])

            sp.wait_ge(scattered, 16 * TOPK * NT)
            with sp.Fori(0, NRB // 2) as i:
                routed(i, 0)
                routed(i, 1)
            for n in range(NRB // 2 * 2, NRB):
                routed(n // 2, n % 2)

        @block.gpsimd
        def _(pool):
            pool.memset(ident[:], 0.0).then_inc(pool_const, 1)
            pool.memset(powexp[:], -0.5).then_inc(pool_const, 1)
            pool.wait_ge(pool_const, 2)
            pool.affine_select(out=ident[:], in_=ident[:], compare_op=ALU.not_equal, fill=1.0, base=0,
                               pattern=[[-1, P]], channel_multiplier=1).then_inc(ident_ok, 1)

            pool.memset(pad_row[:, 0:RW - 2], 0.0).then_inc(pad_ok, 1)
            pool.iota(pad_row[:, RW - 2:RW].bitcast(I32), [[0, 1]], base=T, channel_multiplier=1).then_inc(pad_ok, 1)
            pool.iota(tokens[:], [[P, NT]], base=0, channel_multiplier=1).then_inc(pad_ok, 1)

            def power(n):
                pool.wait_ge(ln_var, n + 1)
                pool.tensor_tensor(rstd[:], veps[:], powexp[:], ALU.pow).then_inc(ln_rstd, 1)

            def pre(b):
                power(max(0, 2 * b - 1))
                pool.wait_ge(dt_log, b + 1)
                for e in range(ET):
                    pool.tensor_tensor(delta[:, b % 2, e, :], delta[:, b % 2, e, :], du[:, b % 2, e, :],
                                       ALU.add).then_inc(delta_ready, 1)
                for e in range(ET):
                    pool.wait_ge(delta_ready, 4 * b + e + 1)
                    pool.tensor_tensor(du[:, b % 2, e, :], delta[:, b % 2, e, :], u[:, b % 2, e, :],
                                       ALU.mult).then_inc(du_ready, 1)

            def scan(b, e):
                pool.wait_ge(du_ready, 4 * b + e + 1)
                first = (4 * b + e) * 8

                def products(q, free):
                    if e == 0:
                        pool.wait_ge(b_ready, q * 16 + 16 * (4 * b + 1))
                    for s in range(2):
                        if free:
                            pool.wait_ge(scan_done, q * 4 + (2 * (first + s) - 2))
                        src = du[:, b % 2, e, :].unsqueeze(1).to_broadcast([P, 2, L])
                        pool.tensor_tensor(dBu[:, s, :, :], src, Bb[:, bass.ds(q * 4 + 2 * s, 2), :],
                                           ALU.mult).then_inc(dbu_ready, 1)

                if first == 0:
                    products(0, False)
                with pool.Fori(0 if first else 1, SG) as q:
                    products(q, True)

            pre(0)
            for b in range(NB):
                scan(b, 0)
                if b:
                    power(2 * b)
                scan(b, 1)
                if b + 1 < NB:
                    pre(b + 1)
                scan(b, 2)
                scan(b, 3)
            power(2 * NB - 1)

            pool.wait_ge(row_ready, NT)
            pool.wait_ge(lg_copied, NT)
            for s in row_stored:
                pool.wait_ge(s, 16 * NT // 2)
            pool.wait_ge(x2_stored, 16 * NT)
            pool.iota(iota_e[:], [[1, E]], base=0, channel_multiplier=0,
                      allow_small_or_imprecise_dtypes=True).then_inc(route_const, 1)
            pool.iota(iota_m[:], [[TB, MAXB]], base=0, channel_multiplier=0,
                      allow_small_or_imprecise_dtypes=True).then_inc(route_const, 1)
            pool.iota(iota_b[:], [[1, NRB]], base=0, channel_multiplier=0,
                      allow_small_or_imprecise_dtypes=True).then_inc(route_const, 1)
            pool.memset(ones[:], 1.0).then_inc(route_const, 1)
            pool.memset(before[:], 1.0).then_inc(route_const, 1)
            pool.memset(keep[:, :, 1:], 1.0).then_inc(route_const, 1)
            pool.memset(keep[:, :, 0:1], 0.0).then_inc(route_const, 1)
            pool.memset(ident16[:], 0.0).then_inc(route_const, 1)
            pool.wait_ge(route_const, 8)
            pool.affine_select(out=ident16[:], in_=ident16[:], compare_op=ALU.not_equal, fill=1.0, base=0,
                               pattern=[[-1, P]], channel_multiplier=1).then_inc(route_const, 1)
            pool.affine_select(out=before[:], in_=before[:], compare_op=ALU.is_gt, fill=0.0, base=0,
                               pattern=[[1, P]], channel_multiplier=-1).then_inc(route_const, 1)

            pool.wait_ge(pad_stored, 32)
            for k in range(TOPK):
                pool.wait_ge(xr_weight, k + 1)
                for t in range(NT):
                    pool.indirect_dma_start(out=slots_dram[:, :],
                                            out_offset=bass.IndirectOffsetOnAxis(ap=slot[:, k, t:t + 1], axis=0),
                                            in_=xr[:, t, :].bitcast(U32), in_offset=None).then_inc(scattered, 16)

            def add(n, s):
                for t in range(BT):
                    pool.wait_ge(y_ok, n * BT + (t + 1))
                    wait(pool, y_added, n * (16 * BT) + 16 * t)
                    pool.sem_inc(add_turns, 1)
                    pool.indirect_dma_start(out=out[:, :],
                                            out_offset=bass.IndirectOffsetOnAxis(ap=dest[:, s, t:t + 1], axis=0),
                                            in_=yb[:, s, t, :], in_offset=None,
                                            compute_op=ALU.add).then_inc(y_added, 16)

            add(0, 0)
            add(1, 1)
            with pool.Fori(1, NBLK // 2) as i:
                add(i * 2, 0)
                add(i * 2 + 1, 1)
            for n in range(NBLK // 2 * 2, NBLK):
                add(n, n % 2)
            pool.wait_ge(y_added, 16 * BT * NBLK)

        @block.scalar
        def _(act):
            def load(b):
                for dst, src, s in ((ctxs[:], ctxT[b], ctx_in), (xs[:, b % 2], x[b], x_in)):
                    act.dma_start(dst, src).then_inc(s, 16)

            load(0)
            act.wait_ge(w_in, 16 * 9)
            act.activation(alog[:], alog[:], ACT.Exp).then_inc(act_const, 1)

            def pre(b):
                act.wait_ge(dve_const, 3)
                if b:
                    act.wait_ge(sz_ready, 4 * b)
                if b >= 2:
                    act.wait_ge(gate_done, 4 * (b - 1))
                for e in range(ET):
                    n = 4 * b + e
                    act.wait_ge(inproj_done, n + 1)
                    if n >= 2:
                        act.wait_ge(u_ready, n - 1)
                    act.activation(xin[:, e % 2, TAPS - 1:], pp[e % 2][:], ACT.Copy)
                    act.activation(cv[:, e % 2, :], pp[e % 2][:], ACT.Identity, bias=cbias[:, e:e + 1],
                                   scale=taps_half[:, e, TAPS - 1:TAPS]).then_inc(xin_ready, 1)
                    if e:
                        tanh_conv(b, e - 1)
                tanh_conv(b, ET - 1)
                act.wait_ge(u_ready, 4 * b + 4)
                for e in range(ET):
                    n = 4 * b + e
                    if e >= 2:
                        act.wait_ge(sz_ready, n - 1)
                    act.wait_ge(z_half, n + 1)
                    act.activation(th[:, e % 2, :], sz[:, b % 2, e, :], ACT.Tanh).then_inc(tanh_z, 1)
                act.wait_ge(xproj_done, b + 1)
                if b:
                    act.wait_ge(bc_stored, 16 * b)
                act.activation(xdbl[:], pp[0][0:DR + 2 * DS, :], ACT.Copy).then_inc(xdbl_ready, 1)
                for e in range(ET):
                    n = 4 * b + e
                    act.wait_ge(dt_done, n + 1)
                    act.activation(delta[:, b % 2, e, :], pp[(e + 1) % 2][:], ACT.Abs, bias=dtbias[:, e:e + 1])
                    act.activation(du[:, b % 2, e, :], pp[(e + 1) % 2][:], ACT.Relu,
                                   bias=dtbias[:, e:e + 1]).then_inc(dt_read, 1)
                act.wait_ge(dt_read, 4 * b + 4)
                act.activation(delta[:, b % 2], delta[:, b % 2], ACT.Exp, scale=-1.0).then_inc(dt_exp, 1)
                act.wait_ge(dt_exp, b + 1)
                act.activation(delta[:, b % 2], delta[:, b % 2], ACT.Ln, bias=1.0).then_inc(dt_log, 1)

            def tanh_conv(b, e):
                act.wait_ge(conv_done, 4 * b + e + 1)
                act.activation(th[:, e % 2, :], cv[:, e % 2, :], ACT.Tanh).then_inc(tanh_u, 1)

            def scan(b, e):
                act.wait_ge(delta_ready, 4 * b + e + 1)
                act.wait_ge(dve_const, 2)
                first = (4 * b + e) * DS

                def decays(q):
                    for r in range(4):
                        if first or not isinstance(q, int) or r >= 2:
                            act.wait_ge(scan_done, q * 4 + (first + r - 1))
                        act.activation(dA[r % 2][:], delta[:, b % 2, e, :], ACT.Exp,
                                       scale=negA[:, bass.ds(q * 4 + (e * DS + r), 1)]).then_inc(dA_ready, 1)

                if first == 0:
                    decays(0)
                with act.Fori(0 if first else 1, SG) as q:
                    decays(q)

            def post(b):
                act.wait_ge(sz_ready, 4 * min(b + 2, NB))
                for c in range(LC):
                    t = LC * b + c
                    act.wait_ge(xn_ready, t + 1)
                    if t >= 2:
                        act.wait_ge(row_stored[c % 2], 16 * (t // 2))
                    act.activation(row[:, c % 2, 0:H], xn[:, c % 2, :], ACT.Copy).then_inc(hi_ready, 1)
                    act.dma_start(out[t * P:(t + 1) * P, :], xs[:, b % 2, c, :]).then_inc(x2_stored, 16)
                    act.wait_ge(xnT_done, t + 1)
                    if t >= 2:
                        act.wait_ge(gate_done, t - 1)
                    act.activation(xnT[:, c % 2, :], pp[c % 2][:], ACT.Copy).then_inc(xnT_copied, 1)
                    act.wait_ge(row_ready, t + 1)
                    act.dma_start(rows_dram[t * P:(t + 1) * P, :], row[:, c % 2, :].bitcast(U32)).then_inc(row_stored[c % 2], 16)

            pre(0)
            act.wait_ge(inproj_done, 4)
            load(1)
            for b in range(NB):
                scan(b, 0)
                if b:
                    post(b - 1)
                    if b + 1 < NB:
                        act.wait_ge(inproj_done, 4 * (b + 1))
                        act.wait_ge(x2_stored, 16 * 4 * b)
                        load(b + 1)
                scan(b, 1)
                if b + 1 < NB:
                    pre(b + 1)
                scan(b, 2)
                scan(b, 3)
            post(NB - 1)
            act.wait_ge(x2_stored, 16 * NT)
            for s in row_stored:
                act.wait_ge(s, 16 * NT // 2)

            act.wait_ge(shifted, 1)
            act.activation(r_exp[:], r_exp[:], ACT.Exp).then_inc(exp_ready, 1)

            def hi_up(n, s, k):
                if k == 0:
                    act.wait_ge(up_in[s], half_count(n, s, 16))
                wait(act, up_done, n * NC - NC)
                act.activation(up_hl[:, s, 0, k, :], up_raw[:, s, k, :], ACT.Copy, scale=WS).then_inc(up_hi, 1)

            def hi_dn(n, s):
                act.wait_ge(dn_in[s], half_count(n, s, 32))
                wait(act, down_done, n * BT - BT)
                act.activation(dn_hl[:, s, 0, 0:2, :], dn_raw[:, s, 0:2, :], ACT.Copy, scale=WS)
                m = IC[-1][1]
                act.activation(dn_hl[0:m, s, 0, 2, :], dn_raw[0:m, s, 2, :], ACT.Copy, scale=WS).then_inc(dn_hi, 1)

            def copy_x(n, s):
                wait(act, up_done, n * NC - NC)
                for t in range(BT):
                    act.wait_ge(xT_done, n * BT + (t + 1))
                    act.activation(xT[:, s, :, t * P:(t + 1) * P], pt[t][:].rearrange("p (k c) -> p k c", c=P),
                                   ACT.Copy).then_inc(xT_copied, 1)

            def silu(n, c):
                act.wait_ge(up_done, n * NC + (c + 1))
                wait(act, a_ok, n * NC + (c + 1 - NC))
                m = IC[c][1]
                act.activation(sg[0:m, c, :], pu[c][0:m, 0:TB], ACT.Silu, scale=1.0 / WS).then_inc(silu_ok, 1)

            def hi_a(n, s, c):
                act.wait_ge(a_ok, n * NC + (c + 1))
                wait(act, down_done, n * BT - BT)
                m = IC[c][1]
                act.activation(a_hl[0:m, s, 0, c, :], a32[0:m, c, :], ACT.Copy).then_inc(a_hi, 1)

            def turn(n, s, more):
                copy_x(n + 1, 1 - s)
                hi_dn(n + 1, 1 - s)
                for c in range(NC):
                    silu(n + 1, c)
                    if more:
                        hi_up(n + 2, s, c)
                        if c == NC - 1:
                            hi_up(n + 2, s, KT - 1)
                    hi_a(n + 1, 1 - s, c)

            for k in range(KT):
                hi_up(0, 0, k)
            hi_dn(0, 0)
            copy_x(0, 0)
            for k in range(KT):
                hi_up(1, 1, k)
            for c in range(NC):
                silu(0, c)
                hi_a(0, 0, c)
            expert_turns(act, turn)

        @block.tensor
        def _(pe):
            def pre(b):
                if b == 0:
                    pe.wait_ge(w_in, 16 * 9)
                pe.wait_ge(ctx_in, 16 * (b + 1))
                if b >= 2:
                    pe.wait_ge(xnT_copied, 4 * (b - 1))
                elif b:
                    pe.wait_ge(dt_read, 4 * b)
                for e in range(ET):
                    n = 4 * b + e
                    if e >= 2:
                        pe.wait_ge(xin_ready, n - 1)
                    for k in range(DM // P):
                        mm = pe.matmul(pp[e % 2][:], inp_w[:, k, e * P:(e + 1) * P], ctxs[:, k, :],
                                       start=(k == 0), stop=(k == DM // P - 1))
                    mm.then_inc(inproj_done, 1)
                pe.wait_ge(u_ready, 4 * b + 4)
                for e in range(ET):
                    mm = pe.matmul(pp[0][0:DR + 2 * DS, :], xp_w[:, e, :], u[:, b % 2, e, :],
                                   start=(e == 0), stop=(e == ET - 1))
                mm.then_inc(xproj_done, 1)
                pe.wait_ge(xdbl_ready, b + 1)
                for e in range(ET):
                    n = 4 * b + e
                    if e >= 2:
                        pe.wait_ge(dt_read, n - 1)
                    pe.matmul(pp[(e + 1) % 2][:], dt_w[:, e * P:(e + 1) * P], xdbl[0:DR, :],
                              start=True, stop=True).then_inc(dt_done, 1)

            def scan(b, e):
                n = 4 * b + e
                first = n * DS
                if n:
                    pe.wait_ge(yv_done, n)
                else:
                    pe.wait_ge(dve_const, 4)
                pe.matmul(yp[:], Ddiag[:, e, :], u[:, b % 2, e, :], start=True, stop=False, skip_group_check=True)
                with pe.Fori(0, SG) as q:
                    for r in range(4):
                        pe.wait_ge(hc_ready, q * 4 + (first + r + 1))
                        pe.matmul(yp[:], ident[:], hc[:, r, :], start=False, stop=False,
                                  skip_group_check=True).then_inc(sum_done, 1)

            def post(b):
                for c in range(LC):
                    t = LC * b + c
                    if c == 0:
                        pe.wait_ge(yv_done, 4 * b + 4)
                        pe.wait_ge(dt_read, 4 * min(b + 2, NB))
                    if c >= 2:
                        pe.wait_ge(x2_ready, t - 1)
                    for e in range(ET):
                        mm = pe.transpose(pp[c % 2][:, e * P:(e + 1) * P], yv[:, e, c * P:(c + 1) * P], ident[:])
                    mm.then_inc(yT_done, 1)
                pe.wait_ge(x2_ready, LC * b + LC)
                for c in range(LC):
                    t = LC * b + c
                    pe.wait_ge(xn_ready, t + 1)
                    if c >= 2:
                        pe.wait_ge(xnT_copied, t - 1)
                    for k in range(H // P):
                        mm = pe.transpose(pp[c % 2][:, k * P:(k + 1) * P], xn[:, c % 2, k * P:(k + 1) * P], ident[:])
                    mm.then_inc(xnT_done, 1)
                    pe.wait_ge(xnT_copied, t + 1)
                    if t:
                        pe.wait_ge(lg_copied, t)
                    for k in range(H // P):
                        mm = pe.matmul(pq[:, 0:E], xnT[:, c % 2, k * P:(k + 1) * P], gate_w[:, k, :],
                                       start=(k == 0), stop=(k == H // P - 1))
                    mm.then_inc(gate_done, 1)

            pe.wait_ge(ident_ok, 1)
            pre(0)
            for b in range(NB):
                scan(b, 0)
                if b:
                    post(b - 1)
                scan(b, 1)
                if b + 1 < NB:
                    pre(b + 1)
                scan(b, 2)
                scan(b, 3)
            post(NB - 1)

            pe.wait_ge(mask_ready, 1)
            pe.wait_ge(route_const, 10)
            flat = picked[:].rearrange("p t e -> p (t e)")
            pe.matmul(pu[0][:, 0:NT * E], before[:], flat, start=True, stop=True)
            pe.matmul(pu[1][:, 0:NT * E], ones[:], flat, start=True, stop=True).then_inc(rank_done, 1)

            def turn_x(n, s):
                pe.wait_ge(rows_in[s], half_count(n, s, 16))
                wait(pe, xT_copied, n * BT)
                for t in range(BT):
                    for k in range(2 * KT):
                        mm = pe.transpose(pt[t][:, k * P:(k + 1) * P], xb[:, s, t, k * P:(k + 1) * P], ident16[:])
                    mm.then_inc(xT_done, 1)

            def up(n, s):
                pe.wait_ge(up_lo, n * KT + KT)
                pe.wait_ge(xT_copied, n * BT + BT)
                for c, (at, m) in enumerate(IC):
                    wait(pe, a_ok, n * NC + (c + 1 - NC))
                    for half in range(2):
                        steps = [(w, v, k) for w, v in ((0, 0), (1, 0), (0, 1)) for k in range(KT)]
                        for j, (w, v, k) in enumerate(steps):
                            mm = pe.matmul(pu[c][0:m, half * TB:(half + 1) * TB],
                                           up_hl[:, s, w, k, half * I + at:half * I + at + m],
                                           xT[:, s, v * KT + k, :], start=(j == 0), stop=(j == len(steps) - 1))
                    mm.then_inc(up_done, 1)

            def down(n, s):
                pe.wait_ge(dn_lo, n + 1)
                pe.wait_ge(a_lo, n * NC + NC)
                for t in range(BT):
                    wait(pe, y_ok, n * BT + (t + 1 - BT))
                    steps = [(c, w, v) for c in range(NC) for w, v in ((0, 0), (1, 0), (0, 1))]
                    for j, (c, w, v) in enumerate(steps):
                        m = IC[c][1]
                        mm = pe.matmul(py[t][:], a_hl[0:m, s, v, c, t * P:(t + 1) * P], dn_hl[0:m, s, w, c, :],
                                       start=(j == 0), stop=(j == len(steps) - 1))
                    mm.then_inc(down_done, 1)

            def turn(n, s, more):
                turn_x(n + 1, 1 - s)
                up(n + 1, 1 - s)
                down(n, s)

            turn_x(0, 0)
            up(0, 0)
            expert_turns(pe, turn)
            down(NBLK - 1, (NBLK - 1) % 2)

        @block.vector
        def _(dve):
            steps = [0]

            def link(ins):
                steps[0] += 1
                ins.then_inc(chain, 1)
                dve.wait_ge(chain, steps[0])

            dve.memset(wshared[:], 1.0 / WS)
            dve.memset(xin[:, :, 0:TAPS - 1], 0.0).then_inc(dve_const, 1)
            dve.wait_ge(act_const, 1)
            dve.tensor_scalar(negA[:], alog[:], -1.0, None, ALU.mult).then_inc(dve_const, 1)
            dve.tensor_scalar(taps_half[:], taps[:], 0.5, None, ALU.mult)
            dve.tensor_scalar(cbias[:], cbias[:], 0.5, None, ALU.mult).then_inc(dve_const, 1)
            dve.wait_ge(ident_ok, 1)
            for e in range(ET):
                ins = dve.tensor_scalar(Ddiag[:, e, :], ident[:], Dcol[:, e:e + 1], None, ALU.mult)
            ins.then_inc(dve_const, 1)
            dve.wait_ge(dve_const, 4)

            def moments(n, tiles):
                for c in range(4):
                    ins = dve.bn_stats(stat[:, c, :], tiles(c))
                link(ins)
                for c in range(4):
                    ins = dve.bn_aggr(mv[:, c, :], stat[:, c, :])
                link(ins)
                dve.tensor_scalar(veps[:], mv[:, :, 1], EPS, None, ALU.add).then_inc(ln_var, 1)
                dve.wait_ge(ln_rstd, n + 1)
                link(dve.scalar_tensor_tensor(out=nmr[:], in0=mv[:, :, 0], scalar=-1.0, in1=rstd[:],
                                              op0=ALU.mult, op1=ALU.mult))

            def pre(b):
                n0 = max(0, 2 * b - 1)
                dve.wait_ge(x_in, 16 * (b + 1))
                moments(n0, lambda c: xs[:, b % 2, c, :])
                link(dve.tensor_scalar(rstd[:], rstd[:], 0.5, None, ALU.mult))
                link(dve.tensor_scalar(nmr[:], nmr[:], 0.5, None, ALU.mult))
                for e in range(ET):
                    n = 4 * b + e
                    dve.wait_ge(xin_ready, n + 1)
                    for k in range(TAPS - 1):
                        ins = dve.scalar_tensor_tensor(out=cv[:, e % 2, :], in0=xin[:, e % 2, k:k + L],
                                                       scalar=taps_half[:, e, k:k + 1], in1=cv[:, e % 2, :],
                                                       op0=ALU.mult, op1=ALU.add)
                        if k < TAPS - 2:
                            link(ins)
                    ins.then_inc(conv_done, 1)
                    dve.tensor_scalar(sz[:, b % 2, e, :], xs[:, b % 2, e, :], rstd[:, e:e + 1], nmr[:, e:e + 1],
                                      ALU.mult, ALU.add).then_inc(z_half, 1)
                    dve.wait_ge(tanh_u, n + 1)
                    dve.scalar_tensor_tensor(out=u[:, b % 2, e, :], in0=th[:, e % 2, :], scalar=1.0,
                                             in1=cv[:, e % 2, :], op0=ALU.add, op1=ALU.mult).then_inc(u_ready, 1)
                for e in range(ET):
                    n = 4 * b + e
                    dve.wait_ge(tanh_z, n + 1)
                    dve.scalar_tensor_tensor(out=sz[:, b % 2, e, :], in0=th[:, e % 2, :], scalar=1.0,
                                             in1=sz[:, b % 2, e, :], op0=ALU.add, op1=ALU.mult).then_inc(sz_ready, 1)

            def scan(b, e):
                first = (4 * b + e) * DS

                def recur(q, r, free=True):
                    dve.wait_ge(dA_ready, q * 4 + (first + r + 1))
                    if r % 2 == 0:
                        dve.wait_ge(dbu_ready, q * 2 + (first // 2 + r // 2 + 1))
                    if free:
                        dve.wait_ge(sum_done, q * 4 + (first + r - 3))
                    dve.tensor_tensor_scan(hc[:, r % 4, :], dA[r % 2][:], dBu[:, (r // 2) % 2, r % 2, :], 0.0,
                                           ALU.mult, ALU.add).then_inc(scan_done, 1)

                def weigh(q, r):
                    dve.wait_ge(scan_done, q * 4 + (first + r + 1))
                    dve.tensor_tensor(hc[:, r, :], hc[:, r, :], Cf[:, bass.ds(q * (4 * L) + r * L, L)],
                                      ALU.mult).then_inc(hc_ready, 1)

                def four(q, last=False):
                    if e == 0:
                        dve.wait_ge(c_ready, q * 16 + 16 * (4 * b + 1))
                    for r in range(4):
                        if not (last and r == 3):
                            recur(q, r + 1, free=first or r == 3 or not isinstance(q, int) or q > 0)
                        weigh(q, r)

                recur(0, 0, free=first > 0)
                if first == 0:
                    four(0)
                with dve.Fori(0 if first else 1, SG - 1) as q:
                    four(q)
                four(SG - 1, last=True)

            def gated(b, e):
                n = 4 * b + e
                dve.wait_ge(sum_done, DS * (n + 1))
                dve.wait_ge(sz_ready, n + 1)
                dve.tensor_tensor(yv[:, e, :], yp[:], sz[:, b % 2, e, :], ALU.mult).then_inc(yv_done, 1)

            def post(b):
                for c in range(LC):
                    t = LC * b + c
                    dve.wait_ge(yT_done, t + 1)
                    ins = dve.tensor_tensor(xs[:, b % 2, c, :], pp[c % 2][:], xs[:, b % 2, c, :], ALU.add)
                    ins.then_inc(x2_ready, 1)
                dve.wait_ge(x2_ready, LC * b + LC)
                moments(2 * b + 2 if b < NB - 1 else 2 * NB - 1, lambda c: xs[:, b % 2, c, :])
                for c in range(LC):
                    t = LC * b + c
                    if t >= 2:
                        dve.wait_ge(xnT_done, t - 1)
                    dve.tensor_scalar(xn[:, c % 2, :], xs[:, b % 2, c, :], rstd[:, c:c + 1], nmr[:, c:c + 1],
                                      ALU.mult, ALU.add).then_inc(xn_ready, 1)
                    dve.wait_ge(hi_ready, t + 1)
                    dve.tensor_copy(row[:, c % 2, RW - 2:RW].bitcast(I32), tokens[:, t:t + 1])
                    dve.tensor_copy(row[:, c % 2, RW - 4:RW - 2].bitcast(F32), wshared[:])
                    dve.tensor_tensor(row[:, c % 2, H:2 * H], xn[:, c % 2, :], row[:, c % 2, 0:H],
                                      ALU.subtract).then_inc(row_ready, 1)
                    dve.wait_ge(gate_done, t + 1)
                    dve.tensor_copy(logits[:, t, :], pq[:, 0:E]).then_inc(lg_copied, 1)

            pre(0)
            for b in range(NB):
                scan(b, 0)
                if b:
                    post(b - 1)
                gated(b, 0)
                scan(b, 1)
                gated(b, 1)
                if b + 1 < NB:
                    pre(b + 1)
                scan(b, 2)
                gated(b, 2)
                scan(b, 3)
                gated(b, 3)
            post(NB - 1)

            def rows3(ap, n):
                return ap.unsqueeze(2).to_broadcast([P, ap.shape[1], n])

            def cols3(ap, n):
                return ap.unsqueeze(1).to_broadcast([P, n, ap.shape[1]])

            for s in row_stored:
                dve.wait_ge(s, 16 * NT // 2)
            dve.wait_ge(x2_stored, 16 * NT)
            dve.wait_ge(lg_copied, NT)
            link(dve.tensor_reduce(r_max[:], logits[:], AX.X, ALU.max))
            dve.tensor_tensor(r_exp[:], logits[:], rows3(r_max[:], E), ALU.subtract).then_inc(shifted, 1)
            dve.memset(g_in[:], -1.0)
            dve.wait_ge(exp_ready, 1)
            link(dve.tensor_reduce(r_sum[:], r_exp[:], AX.X, ALU.add))
            link(dve.reciprocal(r_inv[:], r_sum[:]))
            link(dve.tensor_tensor(score[:], r_exp[:], rows3(r_inv[:], E), ALU.mult))
            link(dve.tensor_reduce(g_in[:, :, 0:G], score[:].rearrange("p t (g j) -> p t g j", g=G), AX.X, ALU.max))
            for t in range(NT):
                ins = dve.max(g_top[:, t, :], g_in[:, t, :])
            link(ins)
            for t in range(NT):
                ins = dve.max_index(g_idx[:, t, :], g_top[:, t, :], g_in[:, t, :])
            dve.wait_ge(route_const, 10)
            link(ins)
            link(dve.tensor_copy(g_idf[:], g_idx[:]))
            dve.tensor_tensor(g_mask[:], cols3(iota_e[:, 0:G], NT), g_idf[:, :, 0:1].to_broadcast([P, NT, G]),
                              ALU.is_equal)
            link(dve.tensor_tensor(g_mask2[:], cols3(iota_e[:, 0:G], NT), g_idf[:, :, 1:2].to_broadcast([P, NT, G]),
                                   ALU.is_equal))
            link(dve.tensor_tensor(g_mask[:], g_mask[:], g_mask2[:], ALU.add))
            link(dve.tensor_tensor(score[:].rearrange("p t (g j) -> p (t g) j", g=G),
                                   score[:].rearrange("p t (g j) -> p (t g) j", g=G),
                                   rows3(g_mask[:].rearrange("p t g -> p (t g)"), E // G), ALU.mult))
            for t in range(NT):
                ins = dve.max(e_top[:, t, :], score[:, t, :])
            link(ins)
            for t in range(NT):
                ins = dve.max_index(e_idx[:, t, :], e_top[:, t, :], score[:, t, :])
            link(ins)
            link(dve.tensor_copy(e_idf[:], e_idx[:]))
            for k in range(TOPK):
                ins = dve.tensor_tensor(onehot[:, k], cols3(iota_e[:], NT),
                                        e_idf[:, :, k:k + 1].to_broadcast([P, NT, E]), ALU.is_equal)
            link(ins)
            link(dve.tensor_tensor(picked[:], onehot[:, 0], onehot[:, 1], ALU.add))
            link(dve.tensor_tensor(picked[:], picked[:], onehot[:, 2], ALU.add))
            dve.tensor_tensor(picked[:], picked[:], onehot[:, 3], ALU.add).then_inc(mask_ready, 1)
            link(dve.tensor_reduce(r_sum[:], e_top[:, :, 0:TOPK], AX.X, ALU.add))
            link(dve.tensor_scalar(r_sum[:], r_sum[:], 1e-20, None, ALU.add))
            link(dve.reciprocal(r_inv[:], r_sum[:]))
            link(dve.tensor_tensor(w_top[:], e_top[:, :, 0:TOPK], rows3(r_inv[:], TOPK), ALU.mult))
            link(dve.tensor_scalar(w_top[:], w_top[:], 1.0 / WS, None, ALU.mult))
            dve.wait_ge(rank_done, 1)
            link(dve.tensor_copy(count[:], pu[1][:, 0:NT * E].rearrange("p (t e) -> p e t", e=E)))
            flat = lambda a: a[:].rearrange("p e t -> p (e t)")
            link(dve.tensor_tensor_scan(flat(cum_t), flat(keep), flat(count), 0.0, ALU.mult, ALU.add))
            link(dve.tensor_tensor(over[:], cum_t[:, :, NT - 1:NT].to_broadcast([P, E, MAXB]), cols3(iota_m[:], E),
                                   ALU.is_gt))
            link(dve.tensor_reduce(nblk[:], over[:], AX.X, ALU.add))
            link(dve.tensor_tensor_scan(cum_b[:], ones[:, 0:E], nblk[:], 0.0, ALU.mult, ALU.add))
            link(dve.tensor_tensor(base[:], cum_b[:], nblk[:], ALU.subtract))
            link(dve.tensor_scalar(base[:], base[:], float(TB), None, ALU.mult))
            link(dve.tensor_tensor(below[:], cols3(cum_b[:], NRB), rows3(iota_b[:], E), ALU.is_le))
            link(dve.tensor_reduce(bexpf[:], below[:], AX.X, ALU.add))
            dve.tensor_scalar(bexp[:], bexpf[:], float(E - 1), None, ALU.min).then_inc(experts_ready, 1)
            link(dve.tensor_tensor(cum_t[:], cum_t[:], count[:], ALU.subtract))
            link(dve.tensor_tensor(cum_t[:], cum_t[:], rows3(base[:], NT), ALU.add))
            link(dve.tensor_tensor(place[:], pu[0][:, 0:NT * E].rearrange("p (t e) -> p t e", e=E),
                                   cum_t[:].rearrange("p e t -> p t e"), ALU.add))
            for k in range(TOPK):
                link(dve.tensor_tensor(prod[:], onehot[:, k], place[:], ALU.mult))
                link(dve.tensor_reduce(slotf[:, k, :], prod[:], AX.X, ALU.add))
            link(dve.tensor_copy(slot[:], slotf[:]))
            dve.wait_ge(xr_in, 16)
            for k in range(TOPK):
                if k:
                    dve.wait_ge(scattered, 16 * NT * k)
                dve.tensor_copy(xr[:, :, RW - 4:RW - 2].bitcast(F32), w_top[:, :, k:k + 1]).then_inc(xr_weight, 1)

            def lo_up(n, s, k):
                dve.wait_ge(up_hi, n * KT + (k + 1))
                wait(dve, up_done, n * NC - NC)
                dve.scalar_tensor_tensor(out=up_hl[:, s, 1, k, :], in0=up_raw[:, s, k, :], scalar=WS,
                                         in1=up_hl[:, s, 0, k, :], op0=ALU.mult,
                                         op1=ALU.subtract).then_inc(up_lo, 1)

            def lo_dn(n, s):
                dve.wait_ge(dn_hi, n + 1)
                m = IC[-1][1]
                dve.scalar_tensor_tensor(out=dn_hl[:, s, 1, 0:2, :], in0=dn_raw[:, s, 0:2, :], scalar=WS,
                                         in1=dn_hl[:, s, 0, 0:2, :], op0=ALU.mult, op1=ALU.subtract)
                dve.scalar_tensor_tensor(out=dn_hl[0:m, s, 1, 2, :], in0=dn_raw[0:m, s, 2, :], scalar=WS,
                                         in1=dn_hl[0:m, s, 0, 2, :], op0=ALU.mult,
                                         op1=ALU.subtract).then_inc(dn_lo, 1)

            def keep_meta(n, s):
                dve.wait_ge(rows_in[s], half_count(n, s, 16))
                dve.tensor_copy(meta[:, bass.ds(n * BT, BT), :],
                                xb[:, s, :, RW - 4:RW].bitcast(U32)).then_inc(meta_ok, 1)

            def gate_up(n, c):
                dve.wait_ge(silu_ok, n * NC + (c + 1))
                wait(dve, a_lo, n * NC + (c + 1 - NC))
                m = IC[c][1]
                dve.scalar_tensor_tensor(out=a32[0:m, c, :], in0=pu[c][0:m, TB:2 * TB], scalar=1.0 / WS,
                                         in1=sg[0:m, c, :], op0=ALU.mult, op1=ALU.mult).then_inc(a_ok, 1)

            def lo_a(n, s, c):
                dve.wait_ge(a_hi, n * NC + (c + 1))
                m = IC[c][1]
                dve.tensor_tensor(a_hl[0:m, s, 1, c, :], a32[0:m, c, :], a_hl[0:m, s, 0, c, :],
                                  ALU.subtract).then_inc(a_lo, 1)

            def weigh_y(n, s):
                wait(dve, y_added, n * (16 * BT) - 16 * BT)
                dve.tensor_copy(dest[:, s, :], meta[:, bass.ds(n * BT, BT), 1])
                for t in range(BT):
                    dve.wait_ge(down_done, n * BT + (t + 1))
                    dve.tensor_scalar(yb[:, s, t, :], py[t][:], meta[:, bass.ds(n * BT + t, 1), 0].bitcast(F32),
                                      None, ALU.mult).then_inc(y_ok, 1)

            def turn(n, s, more, first=False):
                keep_meta(n + 1, 1 - s)
                if not first:
                    weigh_y(n - 1, 1 - s)
                lo_dn(n + 1, 1 - s)
                for c in range(NC):
                    gate_up(n + 1, c)
                    if more:
                        lo_up(n + 2, s, c)
                        if c == NC - 1:
                            lo_up(n + 2, s, KT - 1)
                    lo_a(n + 1, 1 - s, c)

            for k in range(KT):
                lo_up(0, 0, k)
            lo_dn(0, 0)
            keep_meta(0, 0)
            for k in range(KT):
                lo_up(1, 1, k)
            for c in range(NC):
                gate_up(0, c)
                lo_a(0, 0, c)
            expert_turns(dve, lambda n, s, more: turn(n, s, more, first=isinstance(n, int) and n == 0))
            weigh_y(NBLK - 2, NBLK % 2)
            weigh_y(NBLK - 1, (NBLK - 1) % 2)


def kernel(**inputs):
    import numpy as np
    import concourse.bacc as bacc
    from concourse.bass_utils import run_bass_kernel_spmd

    def tiles(a):
        return np.ascontiguousarray(a.reshape((-1, 128) + a.shape[1:]).swapaxes(0, 1))

    up = np.concatenate([inputs["L0_ffn_expert_up_w"],
                         inputs["L0_ffn_shared_up_w"].reshape(2, 2, 352, 512).swapaxes(0, 1).reshape(2, 704, 512)])
    down = np.concatenate([inputs["L0_ffn_expert_down_w"],
                           inputs["L0_ffn_shared_down_w"].reshape(512, 2, 352).swapaxes(0, 1)])
    upT = up.transpose(0, 2, 1).reshape(18, 4, 128, 704).transpose(0, 2, 1, 3)
    downT = down.transpose(0, 2, 1)
    arrays = {
        "x": inputs["x"].reshape(4, 4, 128, 512).transpose(0, 2, 1, 3),
        "ctxT": inputs["ctx_1024"].transpose(0, 2, 1).reshape(4, 2, 128, 512).transpose(0, 2, 1, 3),
        "in_projT": tiles(inputs["L0_xattn_in_proj_w"].T),
        "conv_w": tiles(inputs["L0_xattn_conv_w"]),
        "conv_b": tiles(inputs["L0_xattn_conv_b"]),
        "x_projT": tiles(inputs["L0_xattn_x_proj_w"].T),
        "dt_projT": inputs["L0_xattn_dt_proj_w"].T,
        "dt_b": tiles(inputs["L0_xattn_dt_proj_b"]),
        "A_log": tiles(inputs["L0_xattn_A_log"]).reshape(128, 64),
        "D": tiles(inputs["L0_xattn_D"]),
        "gateT": tiles(inputs["L0_ffn_gate_w"].T),
        "upT": upT,
        "downA": downT[:, :256].reshape(18, 2, 128, 512).transpose(0, 2, 1, 3),
        "downB": downT[:, 256:],
    }
    nc = bacc.Bacc("TRN2", target_bir_lowering=False, num_devices=1)
    feed, args = {}, []
    for name, a in arrays.items():
        a = np.ascontiguousarray(a)
        feed[f"in_{name}"] = a
        args.append(nc.dram_tensor(f"in_{name}", a.shape, mybir.dt.from_np(a.dtype), kind="ExternalInput").ap())
    args.append(nc.dram_tensor("out_0", (2048 + 128, 512), F32, kind="ExternalOutput").ap())
    build(nc, *args)
    got = run_bass_kernel_spmd(nc, [feed], core_ids=[0])
    return got.results[0]["out_0"][:2048].reshape(4, 512, 512)
```

```python
from contextlib import ExitStack

import concourse.bass as bass
from concourse import mybir

F32 = mybir.dt.float32
F16 = mybir.dt.float16
BF16 = mybir.dt.bfloat16
U32 = mybir.dt.uint32
I32 = mybir.dt.int32
ALU = mybir.AluOpType
ACT = mybir.ActivationFunctionType
AX = mybir.AxisListType

P = 128
NB = 4
L = 512
DM = 256
H = 512
DS = 16
DR = 16
TAPS = 4
ET = H // P
LC = L // P
T = NB * L
NT = T // P
E = 16
G = 4
EPS = 1e-5
SG = DS // 4
KT = H // P
I = 352
TOPK = 4
NS = 2
TB = 256
BT = TB // P
NSB = NS * T // TB
MAXT = (T * TOPK + E * (P - 1)) // P
NBIG = (MAXT - E) // 2
NSMALL = max(E, MAXT - 2 * NBIG)
NRB = NBIG + NSMALL
NA = NSB + NBIG - NSMALL
NBLK = NSB + NRB
TILES = 2 * NA + 3 * NSMALL
RW = 2 * H + 4
assert NA % 2 == 0 and NSB % 2 == 0
WS = 64.0
IC = [(c * P, min(P, I - c * P)) for c in range(-(-I // P))]
NC = len(IC)


class Blk:

    def __init__(self, n, s, bt, t, bt_prev):
        self.n, self.s, self.bt, self.t, self.bt_prev = n, s, bt, t, bt_prev
        self.t_prev = t - bt_prev
        self.w = bt * P


def blk(n):
    if n < NA:
        return Blk(n, n % 2, BT, BT * n, BT)
    j, k = divmod(n - NA, 2)
    return Blk(n, k, BT - k, BT * NA + 3 * j + BT * k, BT - 1 if j and k == 0 else BT)


def blk_a(i, k):
    return Blk(i * 2 + k, k % 2, BT, i * (2 * BT) + BT * k, BT)


def blk_b(j, k):
    t = BT * NA + 3 * (k // 2) + BT * (k % 2)
    return Blk(j * 2 + (NA + k), k % 2, BT - k % 2, j * 3 + t, BT - (1 - k % 2))


def build(nc, x, ctxT, in_projT, conv_w, conv_b, x_projT, dt_projT, dt_b, A_log, D, gateT, upT, downA, downB, out):
    bc_dram = nc.dram_tensor("bc_dram", (NB, 2 * DS, L), F32, kind="Internal").ap()
    rows_dram = nc.dram_tensor("rows_dram", (T, RW // 2), U32, kind="Internal").ap()
    slots_dram = nc.dram_tensor("slots_dram", (MAXT * P, RW // 2), U32, kind="Internal").ap()

    with ExitStack() as ctx:
        def sb(name, shape, dt=F32):
            return ctx.enter_context(nc.sbuf_tensor(name, shape, dt))

        def pb(name):
            return ctx.enter_context(nc.psum_tensor(name, [P, 512], F32))

        def sem(name):
            return ctx.enter_context(nc.semaphore(name))

        ident = sb("ident", [P, P])
        inp_w = sb("inp_w", [P, DM // P, H])
        xp_w = sb("xp_w", [P, ET, DR + 2 * DS])
        dt_w = sb("dt_w", [DR, H])
        taps = sb("taps", [P, ET, TAPS])
        taps_half = sb("taps_half", [P, ET, TAPS])
        cbias = sb("cbias", [P, ET])
        dtbias = sb("dtbias", [P, ET])
        alog = sb("alog", [P, ET * DS])
        negA = sb("negA", [P, ET * DS])
        Dcol = sb("Dcol", [P, ET])
        Ddiag = sb("Ddiag", [P, ET, P])
        gate_w = sb("gate_w", [P, H // P, E])
        powexp = sb("powexp", [P, 4])
        logits = sb("logits", [P, NT, E])
        wshared = sb("wshared", [P, 1])
        tokens = sb("tokens", [P, NT], I32)
        pad_row = sb("pad_row", [P, RW], F16)

        scan_mem = ExitStack()

        def sb(name, shape, dt=F32):
            return scan_mem.enter_context(nc.sbuf_tensor(name, shape, dt))

        def pb(name):
            return scan_mem.enter_context(nc.psum_tensor(name, [P, 512], F32))

        Bb = sb("Bb", [P, DS, L])
        Cb = sb("Cb", [P, DS, L])
        Cf = Cb[:].rearrange("p n l -> p (n l)")
        dBu = sb("dBu", [P, 2, 2, L])
        hc = sb("hc", [P, 4, L])
        delta = sb("delta", [P, 2, ET, L])
        u = sb("u", [P, 2, ET, L])
        du = sb("du", [P, 2, ET, L])
        xs = sb("xs", [P, 2, LC, H])
        ctxs = sb("ctxs", [P, DM // P, L])
        sz = sb("sz", [P, 2, ET, L])
        xin = sb("xin", [P, 2, L + TAPS - 1])
        cv = sb("cv", [P, 2, L])
        th = sb("th", [P, 2, L])
        xdbl = sb("xdbl", [DR + 2 * DS, L])
        yv = sb("yv", [P, ET, L])
        xn = sb("xn", [P, 2, H])
        xnT = th
        row = sb("row", [P, 2, RW], F16)
        stat = sb("stat", [P, 4, 6])
        mv = sb("mv", [P, 4, 2])
        veps = sb("veps", [P, 4])
        rstd = sb("rstd", [P, 4])
        nmr = sb("nmr", [P, 4])

        dA = [pb(f"dA{i}") for i in range(2)]
        yp = pb("yp")
        pp = [pb(f"pp{i}") for i in range(2)]
        pq = pb("pq")
        scan_mem.close()

        def sb(name, shape, dt=F32):
            return ctx.enter_context(nc.sbuf_tensor(name, shape, dt))

        ident16 = sb("ident16", [P, P], F16)
        up_raw = sb("up_raw", [P, 2, KT, 2 * I])
        dn_raw = sb("dn_raw", [P, 2, NC, H])
        up_hl = sb("up_hl", [P, 2, 2, KT, 2 * I], F16)
        dn_hl = sb("dn_hl", [P, 2, 2, NC, H], F16)
        xb = sb("xb", [P, 2, BT, RW], F16)
        xT = sb("xT", [P, 2, 2 * KT, TB], F16)
        sg = sb("sg", [P, NC, TB])
        a32 = sb("a32", [P, NC, TB])
        a_hl = sb("a_hl", [P, 2, 2, NC, TB], F16)
        yb = sb("yb", [P, 2, BT, H])
        meta = sb("meta", [P, TILES, 2], U32)
        dest = sb("dest", [P, 2, BT], U32)
        xr = sb("xr", [P, NT, RW], F16)
        r_max = sb("r_max", [P, NT])
        r_exp = sb("r_exp", [P, NT, E])
        r_sum = sb("r_sum", [P, NT])
        r_inv = sb("r_inv", [P, NT])
        score = sb("score", [P, NT, E])
        g_in = sb("g_in", [P, NT, 8])
        g_top = sb("g_top", [P, NT, 8])
        g_idx = sb("g_idx", [P, NT, 8], U32)
        g_idf = sb("g_idf", [P, NT, 8])
        g_mask = sb("g_mask", [P, NT, G])
        g_mask2 = sb("g_mask2", [P, NT, G])
        e_top = sb("e_top", [P, NT, 8])
        e_idx = sb("e_idx", [P, NT, 8], U32)
        e_idf = sb("e_idf", [P, NT, 8])
        w_top = sb("w_top", [P, NT, TOPK])
        onehot = sb("onehot", [P, TOPK, NT, E])
        picked = sb("picked", [P, NT, E])
        count = sb("count", [P, E, NT])
        cum_t = sb("cum_t", [P, E, NT])
        over = sb("over", [P, E, NT])
        tiles_e = sb("tiles_e", [P, E])
        big_e = sb("big_e", [P, E])
        big_to = sb("big_to", [P, E])
        big_from = sb("big_from", [P, E])
        small_e = sb("small_e", [P, E])
        small_to = sb("small_to", [P, E])
        in_big = sb("in_big", [P, E])
        to_small = sb("to_small", [P, E])
        rank = sb("rank", [P, NT, E])
        place = sb("place", [P, NT, E])
        prod = sb("prod", [P, NT, E])
        slotf = sb("slotf", [P, TOPK, NT])
        slot = sb("slot", [P, TOPK, NT], U32)
        below = sb("below", [P, NRB, E])
        bexpf = sb("bexpf", [P, NRB])
        bexp = sb("bexp", [P, NRB], I32)
        iota_e = sb("iota_e", [P, E])
        iota_m = sb("iota_m", [P, NT])
        iota_b = sb("iota_b", [P, NRB])
        keep = sb("keep", [P, E, NT])
        ones = sb("ones", [P, P])
        before = sb("before", [P, P])

        def pb(name, shape=(P, 512), dt=F32):
            return ctx.enter_context(nc.psum_tensor(name, list(shape), dt))

        pt = [pb(f"pt{i}", (P, 2 * KT * P), F16) for i in range(BT)]
        pu = [pb(f"pu{i}") for i in range(NC)]
        py = [pb(f"py{i}") for i in range(BT)]

        w_in = sem("w_in")
        ctx_in = sem("ctx_in")
        x_in = sem("x_in")
        ident_ok = sem("ident_ok")
        pool_const = sem("pool_const")
        act_const = sem("act_const")
        dve_const = sem("dve_const")
        chain = sem("chain")
        inproj_done = sem("inproj_done")
        xin_ready = sem("xin_ready")
        conv_done = sem("conv_done")
        tanh_u = sem("tanh_u")
        u_ready = sem("u_ready")
        xproj_done = sem("xproj_done")
        xdbl_ready = sem("xdbl_ready")
        bc_stored = sem("bc_stored")
        b_ready = sem("b_ready")
        c_ready = sem("c_ready")
        dt_done = sem("dt_done")
        dt_read = sem("dt_read")
        dt_exp = sem("dt_exp")
        dt_log = sem("dt_log")
        delta_ready = sem("delta_ready")
        du_ready = sem("du_ready")
        ln_var = sem("ln_var")
        ln_rstd = sem("ln_rstd")
        ln_shift = sem("ln_shift")
        z_half = sem("z_half")
        tanh_z = sem("tanh_z")
        sz_ready = sem("sz_ready")
        dA_ready = sem("dA_ready")
        dbu_ready = sem("dbu_ready")
        scan_done = sem("scan_done")
        hc_ready = sem("hc_ready")
        sum_done = sem("sum_done")
        yv_done = sem("yv_done")
        yT_done = sem("yT_done")
        x2_ready = sem("x2_ready")
        xn_ready = sem("xn_ready")
        hi_ready = sem("hi_ready")
        row_ready = sem("row_ready")
        xnT_done = sem("xnT_done")
        xnT_copied = sem("xnT_copied")
        gate_done = sem("gate_done")
        lg_copied = sem("lg_copied")
        x2_stored = sem("x2_stored")
        row_stored = [sem(f"row_stored{i}") for i in range(2)]


        pad_ok = sem("pad_ok")
        pad_stored = sem("pad_stored")
        route_const = sem("route_const")
        shifted = sem("shifted")
        exp_ready = sem("exp_ready")
        mask_ready = sem("mask_ready")
        rank_done = sem("rank_done")
        rank_read = sem("rank_read")
        experts_ready = sem("experts_ready")
        xr_in = sem("xr_in")
        slot_ok = sem("slot_ok")
        xr_weight = sem("xr_weight")
        scattered = sem("scattered")
        up_in = [sem(f"up_in{i}") for i in range(2)]
        dn_in = [sem(f"dn_in{i}") for i in range(2)]
        rows_in = [sem(f"rows_in{i}") for i in range(2)]
        up_hi = sem("up_hi")
        up_lo = sem("up_lo")
        dn_hi = sem("dn_hi")
        dn_lo = sem("dn_lo")
        meta_ok = sem("meta_ok")
        xT_done = sem("xT_done")
        xT_copied = sem("xT_copied")
        up_done = sem("up_done")
        silu_ok = sem("silu_ok")
        a_ok = sem("a_ok")
        a_hi = sem("a_hi")
        a_lo = sem("a_lo")
        down_done = sem("down_done")
        y_ok = sem("y_ok")
        y_added = sem("y_added")
        add_turns = sem("add_turns")

        def wait(eng, s, v):
            if not isinstance(v, int) or v > 0:
                eng.wait_ge(s, v)

        def half_count(n, s, step):
            if isinstance(n, int):
                return step * (n // 2 + 1)
            return n * (step // 2) + (step - s * (step // 2))

        def expert_turns(turn, fori):
            def at(n):
                return blk(n) if n < NBLK else None

            def peeled(lo, hi):
                for n in range(lo, hi):
                    turn(at(n), at(n + 1), at(n + 2))

            peeled(0, 2)
            with fori(1, NA // 2 - 1) as i:
                for k in range(2):
                    turn(blk_a(i, k), blk_a(i, k + 1), blk_a(i, k + 2))
            peeled(NA - 2, NA + 2)
            with fori(1, NSMALL - 1) as j:
                for k in range(2):
                    turn(blk_b(j, k), blk_b(j, k + 1), blk_b(j, k + 2))
            peeled(NBLK - 2, NBLK)

        block = ctx.enter_context(nc.Block())

        @block.sync
        def _(sp):
            for dst, src in ((inp_w[:], in_projT), (xp_w[:], x_projT), (dt_w[:], dt_projT), (taps[:], conv_w),
                             (cbias[:], conv_b), (dtbias[:], dt_b), (alog[:], A_log), (Dcol[:], D),
                             (gate_w[:], gateT)):
                sp.dma_start(dst, src).then_inc(w_in, 16)
            sp.wait_ge(pad_ok, 3)
            sp.dma_start(slots_dram.rearrange("(n p) c -> p n c", p=P),
                         pad_row[:].bitcast(U32).unsqueeze(1).to_broadcast([P, MAXT, RW // 2])).then_inc(pad_stored, 16)
            sp.dma_start(out[T:, :], pad_row[:, 0:2 * H].bitcast(F32)).then_inc(pad_stored, 16)
            for b in range(NB):
                sp.wait_ge(xdbl_ready, b + 1)
                sp.dma_start(bc_dram[b], xdbl[DR:, :]).then_inc(bc_stored, 16)
                sp.wait_ge(bc_stored, 16 * (b + 1))
                for q in range(SG):
                    if b:
                        sp.wait_ge(dbu_ready, 8 * (4 * b - 1) + 2 * q + 2)
                    sp.dma_start(Bb[:, 4 * q:4 * q + 4, :],
                                 bc_dram[b, 4 * q:4 * q + 4, :].partition_broadcast(P)).then_inc(b_ready, 16)
                    if b:
                        sp.wait_ge(hc_ready, 16 * (4 * b - 1) + 4 * q + 4)
                    sp.dma_start(Cb[:, 4 * q:4 * q + 4, :],
                                 bc_dram[b, DS + 4 * q:DS + 4 * q + 4, :].partition_broadcast(P)).then_inc(c_ready, 16)
                    sp.wait_ge(b_ready, 16 * (4 * b + q + 1))
                    sp.wait_ge(c_ready, 16 * (4 * b + q + 1))

            sp.wait_ge(row_ready, NT)
            sp.wait_ge(lg_copied, NT)
            for s in row_stored:
                sp.wait_ge(s, 16 * NT // 2)
            sp.wait_ge(x2_stored, 16 * NT)
            def load_up(b, e):
                wait(sp, up_lo, b.n * KT - KT)
                sp.dma_start(up_raw[:, b.s], upT[bass.ds(e, 1)].squeeze(0)).then_inc(up_in[b.s], 16)

            def load_dn(b, e):
                wait(sp, dn_lo, b.n - 1)
                sp.dma_start(dn_raw[:, b.s, 0:2, :], downA[bass.ds(e, 1)].squeeze(0)).then_inc(dn_in[b.s], 16)
                sp.dma_start(dn_raw[0:IC[-1][1], b.s, 2, :], downB[bass.ds(e, 1)].squeeze(0)).then_inc(dn_in[b.s], 16)

            def load_rows(b, src):
                wait(sp, xT_done, b.t_prev)
                wait(sp, meta_ok, b.n - 1)
                sp.dma_start(xb[:, b.s, 0:b.bt].bitcast(U32),
                             src.rearrange("(t p) c -> p t c", p=P)).then_inc(rows_in[b.s], 16)

            half = NSB // NS
            for h in range(NS):
                def shared(i):
                    for s in range(2):
                        b = blk_a(i, h * half + s)
                        load_up(b, E + h)
                        load_dn(b, E + h)
                        load_rows(b, rows_dram[bass.ds(i * (2 * TB) + s * TB, TB), :])
                if h == 0:
                    shared(0)
                    sp.dma_start(xr[:].bitcast(U32), rows_dram.rearrange("(t p) c -> p t c", p=P)).then_inc(xr_in, 16)
                with sp.Fori(1 - h, half // 2) as i:
                    shared(i)
            sp.wait_ge(experts_ready, 1)

            def routed(b, at, row):
                e = sp.value_load(bexp[0:1, bass.ds(at, 1)], min_val=0, max_val=E - 1)
                load_up(b, e)
                load_dn(b, e)
                load_rows(b, slots_dram[bass.ds(row, b.w), :])

            sp.wait_ge(scattered, 16 * TOPK * NT)
            with sp.Fori(0, (NA - NSB) // 2) as i:
                for s in range(2):
                    routed(blk_a(i, NSB + s), i * 2 + s, i * (2 * TB) + s * TB)

            def big_small(j, big, small):
                routed(big, j + (NA - NSB), j * TB + (NA - NSB) * TB)
                routed(small, j + NBIG, j * P + NBIG * TB)

            big_small(0, blk(NA), blk(NA + 1))
            with sp.Fori(1, NSMALL) as j:
                big_small(j, blk_b(j, 0), blk_b(j, 1))

        @block.gpsimd
        def _(pool):
            pool.memset(ident[:], 0.0).then_inc(pool_const, 1)
            pool.memset(powexp[:], -0.5).then_inc(pool_const, 1)
            pool.wait_ge(pool_const, 2)
            pool.affine_select(out=ident[:], in_=ident[:], compare_op=ALU.not_equal, fill=1.0, base=0,
                               pattern=[[-1, P]], channel_multiplier=1).then_inc(ident_ok, 1)

            pool.memset(pad_row[:, 0:RW - 2], 0.0).then_inc(pad_ok, 1)
            pool.iota(pad_row[:, RW - 2:RW].bitcast(I32), [[0, 1]], base=T, channel_multiplier=1).then_inc(pad_ok, 1)
            pool.iota(tokens[:], [[P, NT]], base=0, channel_multiplier=1).then_inc(pad_ok, 1)

            def power(n):
                pool.wait_ge(ln_var, n + 1)
                pool.tensor_tensor(rstd[:], veps[:], powexp[:], ALU.pow).then_inc(ln_rstd, 1)

            def pre(b):
                power(max(0, 2 * b - 1))
                pool.wait_ge(dt_log, b + 1)
                for e in range(ET):
                    pool.tensor_tensor(delta[:, b % 2, e, :], delta[:, b % 2, e, :], du[:, b % 2, e, :],
                                       ALU.add).then_inc(delta_ready, 1)
                for e in range(ET):
                    pool.wait_ge(delta_ready, 4 * b + e + 1)
                    pool.tensor_tensor(du[:, b % 2, e, :], delta[:, b % 2, e, :], u[:, b % 2, e, :],
                                       ALU.mult).then_inc(du_ready, 1)

            def scan(b, e):
                pool.wait_ge(du_ready, 4 * b + e + 1)
                first = (4 * b + e) * 8

                def products(q, free):
                    if e == 0:
                        pool.wait_ge(b_ready, q * 16 + 16 * (4 * b + 1))
                    for s in range(2):
                        if free:
                            pool.wait_ge(scan_done, q * 4 + (2 * (first + s) - 2))
                        src = du[:, b % 2, e, :].unsqueeze(1).to_broadcast([P, 2, L])
                        pool.tensor_tensor(dBu[:, s, :, :], src, Bb[:, bass.ds(q * 4 + 2 * s, 2), :],
                                           ALU.mult).then_inc(dbu_ready, 1)

                if first == 0:
                    products(0, False)
                with pool.Fori(0 if first else 1, SG) as q:
                    products(q, True)

            pre(0)
            for b in range(NB):
                scan(b, 0)
                if b:
                    power(2 * b)
                scan(b, 1)
                if b + 1 < NB:
                    pre(b + 1)
                scan(b, 2)
                scan(b, 3)
            power(2 * NB - 1)

            pool.wait_ge(row_ready, NT)
            pool.wait_ge(lg_copied, NT)
            for s in row_stored:
                pool.wait_ge(s, 16 * NT // 2)
            pool.wait_ge(x2_stored, 16 * NT)
            pool.iota(iota_e[:], [[1, E]], base=0, channel_multiplier=0,
                      allow_small_or_imprecise_dtypes=True).then_inc(route_const, 1)
            pool.iota(iota_m[:], [[P, NT]], base=0, channel_multiplier=0,
                      allow_small_or_imprecise_dtypes=True).then_inc(route_const, 1)
            pool.iota(iota_b[:], [[1, NRB]], base=0, channel_multiplier=0,
                      allow_small_or_imprecise_dtypes=True).then_inc(route_const, 1)
            pool.memset(ones[:], 1.0).then_inc(route_const, 1)
            pool.memset(before[:], 1.0).then_inc(route_const, 1)
            pool.memset(keep[:, :, 1:], 1.0).then_inc(route_const, 1)
            pool.memset(keep[:, :, 0:1], 0.0).then_inc(route_const, 1)
            pool.memset(ident16[:], 0.0).then_inc(route_const, 1)
            pool.wait_ge(route_const, 8)
            pool.affine_select(out=ident16[:], in_=ident16[:], compare_op=ALU.not_equal, fill=1.0, base=0,
                               pattern=[[-1, P]], channel_multiplier=1).then_inc(route_const, 1)
            pool.affine_select(out=before[:], in_=before[:], compare_op=ALU.is_gt, fill=0.0, base=0,
                               pattern=[[1, P]], channel_multiplier=-1).then_inc(route_const, 1)

            def scatter(k, tiles):
                for t in tiles:
                    pool.indirect_dma_start(out=slots_dram[:, :],
                                            out_offset=bass.IndirectOffsetOnAxis(ap=slot[:, k, t:t + 1], axis=0),
                                            in_=xr[:, t, :].bitcast(U32), in_offset=None).then_inc(scattered, 16)

            def add(b):
                for t in range(b.bt):
                    pool.wait_ge(y_ok, b.t + (t + 1))
                    wait(pool, y_added, b.t * 16 + 16 * t)
                    pool.sem_inc(add_turns, 1)
                    pool.indirect_dma_start(out=out[:, :],
                                            out_offset=bass.IndirectOffsetOnAxis(ap=dest[:, b.s, t:t + 1], axis=0),
                                            in_=yb[:, b.s, t, :], in_offset=None,
                                            compute_op=ALU.add).then_inc(y_added, 16)

            pool.wait_ge(pad_stored, 32)
            pool.wait_ge(xr_in, 16)
            pool.wait_ge(slot_ok, 1)
            for n in range(2 * TOPK):
                k = n // 2
                if n % 2 == 0:
                    if k:
                        pool.wait_ge(scattered, 16 * NT * k)
                    pool.tensor_copy(xr[:, :, RW - 4:RW - 2].bitcast(F32), w_top[:, :, k:k + 1]).then_inc(xr_weight, 1)
                    pool.wait_ge(xr_weight, k + 1)
                scatter(k, range(NT // 2 * (n % 2), NT // 2 * (n % 2 + 1)))
                add(blk(n))
            with pool.Fori(TOPK, NA // 2) as i:
                for k in range(2):
                    add(blk_a(i, k))
            for n in range(NA, NA + 2):
                add(blk(n))
            with pool.Fori(1, NSMALL) as j:
                for k in range(2):
                    add(blk_b(j, k))
            pool.wait_ge(y_added, 16 * TILES)

        @block.scalar
        def _(act):
            def load(b):
                for dst, src, s in ((ctxs[:], ctxT[b], ctx_in), (xs[:, b % 2], x[b], x_in)):
                    act.dma_start(dst, src).then_inc(s, 16)

            load(0)
            act.wait_ge(w_in, 16 * 9)
            act.activation(alog[:], alog[:], ACT.Exp).then_inc(act_const, 1)

            def pre(b):
                act.wait_ge(dve_const, 3)
                if b:
                    act.wait_ge(sz_ready, 4 * b)
                if b >= 2:
                    act.wait_ge(gate_done, 4 * (b - 1))
                for e in range(ET):
                    n = 4 * b + e
                    act.wait_ge(inproj_done, n + 1)
                    if n >= 2:
                        act.wait_ge(u_ready, n - 1)
                    act.activation(xin[:, e % 2, TAPS - 1:], pp[e % 2][:], ACT.Copy)
                    act.activation(cv[:, e % 2, :], pp[e % 2][:], ACT.Identity, bias=cbias[:, e:e + 1],
                                   scale=taps_half[:, e, TAPS - 1:TAPS]).then_inc(xin_ready, 1)
                    if e:
                        tanh_conv(b, e - 1)
                tanh_conv(b, ET - 1)
                act.wait_ge(u_ready, 4 * b + 4)
                for e in range(ET):
                    n = 4 * b + e
                    if e >= 2:
                        act.wait_ge(sz_ready, n - 1)
                    act.wait_ge(z_half, n + 1)
                    act.activation(th[:, e % 2, :], sz[:, b % 2, e, :], ACT.Tanh).then_inc(tanh_z, 1)
                act.wait_ge(xproj_done, b + 1)
                if b:
                    act.wait_ge(bc_stored, 16 * b)
                act.activation(xdbl[:], pp[0][0:DR + 2 * DS, :], ACT.Copy).then_inc(xdbl_ready, 1)
                for e in range(ET):
                    n = 4 * b + e
                    act.wait_ge(dt_done, n + 1)
                    act.activation(delta[:, b % 2, e, :], pp[(e + 1) % 2][:], ACT.Abs, bias=dtbias[:, e:e + 1])
                    act.activation(du[:, b % 2, e, :], pp[(e + 1) % 2][:], ACT.Relu,
                                   bias=dtbias[:, e:e + 1]).then_inc(dt_read, 1)
                act.wait_ge(dt_read, 4 * b + 4)
                act.activation(delta[:, b % 2], delta[:, b % 2], ACT.Exp, scale=-1.0).then_inc(dt_exp, 1)
                act.wait_ge(dt_exp, b + 1)
                act.activation(delta[:, b % 2], delta[:, b % 2], ACT.Ln, bias=1.0).then_inc(dt_log, 1)

            def tanh_conv(b, e):
                act.wait_ge(conv_done, 4 * b + e + 1)
                act.activation(th[:, e % 2, :], cv[:, e % 2, :], ACT.Tanh).then_inc(tanh_u, 1)

            def scan(b, e):
                act.wait_ge(delta_ready, 4 * b + e + 1)
                act.wait_ge(dve_const, 2)
                first = (4 * b + e) * DS

                def decays(q):
                    for r in range(4):
                        if first or not isinstance(q, int) or r >= 2:
                            act.wait_ge(scan_done, q * 4 + (first + r - 1))
                        act.activation(dA[r % 2][:], delta[:, b % 2, e, :], ACT.Exp,
                                       scale=negA[:, bass.ds(q * 4 + (e * DS + r), 1)]).then_inc(dA_ready, 1)

                if first == 0:
                    decays(0)
                with act.Fori(0 if first else 1, SG) as q:
                    decays(q)

            def post(b):
                act.wait_ge(sz_ready, 4 * min(b + 2, NB))
                for c in range(LC):
                    t = LC * b + c
                    act.wait_ge(xn_ready, t + 1)
                    if t >= 2:
                        act.wait_ge(row_stored[c % 2], 16 * (t // 2))
                    act.activation(row[:, c % 2, 0:H], xn[:, c % 2, :], ACT.Copy).then_inc(hi_ready, 1)
                    act.dma_start(out[t * P:(t + 1) * P, :], xs[:, b % 2, c, :]).then_inc(x2_stored, 16)
                    act.wait_ge(xnT_done, t + 1)
                    if t >= 2:
                        act.wait_ge(gate_done, t - 1)
                    act.activation(xnT[:, c % 2, :], pp[c % 2][:], ACT.Copy).then_inc(xnT_copied, 1)
                    act.wait_ge(row_ready, t + 1)
                    act.dma_start(rows_dram[t * P:(t + 1) * P, :], row[:, c % 2, :].bitcast(U32)).then_inc(row_stored[c % 2], 16)

            pre(0)
            act.wait_ge(inproj_done, 4)
            load(1)
            for b in range(NB):
                scan(b, 0)
                if b:
                    post(b - 1)
                    if b + 1 < NB:
                        act.wait_ge(inproj_done, 4 * (b + 1))
                        act.wait_ge(x2_stored, 16 * 4 * b)
                        load(b + 1)
                scan(b, 1)
                if b + 1 < NB:
                    pre(b + 1)
                scan(b, 2)
                scan(b, 3)
            post(NB - 1)
            act.wait_ge(x2_stored, 16 * NT)
            for s in row_stored:
                act.wait_ge(s, 16 * NT // 2)

            def hi_up(b, k):
                if k == 0:
                    act.wait_ge(up_in[b.s], half_count(b.n, b.s, 16))
                wait(act, up_done, b.n * NC - NC)
                act.activation(up_hl[:, b.s, 0, k, :], up_raw[:, b.s, k, :], ACT.Copy, scale=WS).then_inc(up_hi, 1)

            def hi_dn(b):
                act.wait_ge(dn_in[b.s], half_count(b.n, b.s, 32))
                wait(act, down_done, b.t_prev)
                act.activation(dn_hl[:, b.s, 0, 0:2, :], dn_raw[:, b.s, 0:2, :], ACT.Copy, scale=WS)
                m = IC[-1][1]
                act.activation(dn_hl[0:m, b.s, 0, 2, :], dn_raw[0:m, b.s, 2, :], ACT.Copy, scale=WS).then_inc(dn_hi, 1)

            def copy_x(b):
                wait(act, up_done, b.n * NC - NC)
                for t in range(b.bt):
                    act.wait_ge(xT_done, b.t + (t + 1))
                    act.activation(xT[:, b.s, :, t * P:(t + 1) * P], pt[t][:].rearrange("p (k c) -> p k c", c=P),
                                   ACT.Copy).then_inc(xT_copied, 1)

            def silu(b, c):
                act.wait_ge(up_done, b.n * NC + (c + 1))
                wait(act, a_ok, b.n * NC + (c + 1 - NC))
                m = IC[c][1]
                act.activation(sg[0:m, c, 0:b.w], pu[c][0:m, 0:b.w], ACT.Silu, scale=1.0 / WS).then_inc(silu_ok, 1)

            def hi_a(b, c):
                act.wait_ge(a_ok, b.n * NC + (c + 1))
                wait(act, down_done, b.t_prev)
                m = IC[c][1]
                act.activation(a_hl[0:m, b.s, 0, c, 0:b.w], a32[0:m, c, 0:b.w], ACT.Copy).then_inc(a_hi, 1)

            def turn(cur, nxt, after):
                if nxt is None:
                    return
                hi_dn(nxt)
                if after:
                    hi_up(after, 0)
                for c in range(NC):
                    silu(nxt, c)
                    if after and c + 1 < KT:
                        hi_up(after, c + 1)
                    hi_a(nxt, c)
                if after:
                    copy_x(after)

            for k in range(KT):
                hi_up(blk(0), k)
            copy_x(blk(0))
            hi_dn(blk(0))
            act.wait_ge(shifted, 1)
            act.activation(r_exp[:], r_exp[:], ACT.Exp).then_inc(exp_ready, 1)
            for k in range(KT):
                hi_up(blk(1), k)
            for c in range(NC):
                silu(blk(0), c)
                hi_a(blk(0), c)
            copy_x(blk(1))
            expert_turns(turn, act.Fori)

        @block.tensor
        def _(pe):
            def pre(b):
                if b == 0:
                    pe.wait_ge(w_in, 16 * 9)
                pe.wait_ge(ctx_in, 16 * (b + 1))
                if b >= 2:
                    pe.wait_ge(xnT_copied, 4 * (b - 1))
                elif b:
                    pe.wait_ge(dt_read, 4 * b)
                for e in range(ET):
                    n = 4 * b + e
                    if e >= 2:
                        pe.wait_ge(xin_ready, n - 1)
                    for k in range(DM // P):
                        mm = pe.matmul(pp[e % 2][:], inp_w[:, k, e * P:(e + 1) * P], ctxs[:, k, :],
                                       start=(k == 0), stop=(k == DM // P - 1))
                    mm.then_inc(inproj_done, 1)
                pe.wait_ge(u_ready, 4 * b + 4)
                for e in range(ET):
                    mm = pe.matmul(pp[0][0:DR + 2 * DS, :], xp_w[:, e, :], u[:, b % 2, e, :],
                                   start=(e == 0), stop=(e == ET - 1))
                mm.then_inc(xproj_done, 1)
                pe.wait_ge(xdbl_ready, b + 1)
                for e in range(ET):
                    n = 4 * b + e
                    if e >= 2:
                        pe.wait_ge(dt_read, n - 1)
                    pe.matmul(pp[(e + 1) % 2][:], dt_w[:, e * P:(e + 1) * P], xdbl[0:DR, :],
                              start=True, stop=True).then_inc(dt_done, 1)

            def scan(b, e):
                n = 4 * b + e
                first = n * DS
                if n:
                    pe.wait_ge(yv_done, n)
                else:
                    pe.wait_ge(dve_const, 4)
                pe.matmul(yp[:], Ddiag[:, e, :], u[:, b % 2, e, :], start=True, stop=False, skip_group_check=True)
                with pe.Fori(0, SG) as q:
                    for r in range(4):
                        pe.wait_ge(hc_ready, q * 4 + (first + r + 1))
                        pe.matmul(yp[:], ident[:], hc[:, r, :], start=False, stop=False,
                                  skip_group_check=True).then_inc(sum_done, 1)

            def post(b):
                for c in range(LC):
                    t = LC * b + c
                    if c == 0:
                        pe.wait_ge(yv_done, 4 * b + 4)
                        pe.wait_ge(dt_read, 4 * min(b + 2, NB))
                    if c >= 2:
                        pe.wait_ge(x2_ready, t - 1)
                    for e in range(ET):
                        mm = pe.transpose(pp[c % 2][:, e * P:(e + 1) * P], yv[:, e, c * P:(c + 1) * P], ident[:])
                    mm.then_inc(yT_done, 1)
                pe.wait_ge(x2_ready, LC * b + LC)
                for c in range(LC):
                    t = LC * b + c
                    pe.wait_ge(xn_ready, t + 1)
                    if c >= 2:
                        pe.wait_ge(xnT_copied, t - 1)
                    for k in range(H // P):
                        mm = pe.transpose(pp[c % 2][:, k * P:(k + 1) * P], xn[:, c % 2, k * P:(k + 1) * P], ident[:])
                    mm.then_inc(xnT_done, 1)
                    pe.wait_ge(xnT_copied, t + 1)
                    if t:
                        pe.wait_ge(lg_copied, t)
                    for k in range(H // P):
                        mm = pe.matmul(pq[:, 0:E], xnT[:, c % 2, k * P:(k + 1) * P], gate_w[:, k, :],
                                       start=(k == 0), stop=(k == H // P - 1))
                    mm.then_inc(gate_done, 1)

            pe.wait_ge(ident_ok, 1)
            pre(0)
            for b in range(NB):
                scan(b, 0)
                if b:
                    post(b - 1)
                scan(b, 1)
                if b + 1 < NB:
                    pre(b + 1)
                scan(b, 2)
                scan(b, 3)
            post(NB - 1)

            def turn_x(b):
                pe.wait_ge(rows_in[b.s], half_count(b.n, b.s, 16))
                wait(pe, xT_copied, b.t)
                for t in range(b.bt):
                    for k in range(2 * KT):
                        mm = pe.transpose(pt[t][:, k * P:(k + 1) * P], xb[:, b.s, t, k * P:(k + 1) * P], ident16[:])
                    mm.then_inc(xT_done, 1)

            def up(b):
                pe.wait_ge(up_lo, b.n * KT + KT)
                pe.wait_ge(xT_copied, b.t + b.bt)
                for c, (at, m) in enumerate(IC):
                    wait(pe, a_ok, b.n * NC + (c + 1 - NC))
                    for half in range(2):
                        steps = [(w, v, k) for w, v in ((0, 0), (1, 0), (0, 1)) for k in range(KT)]
                        for j, (w, v, k) in enumerate(steps):
                            mm = pe.matmul(pu[c][0:m, half * TB:half * TB + b.w],
                                           up_hl[:, b.s, w, k, half * I + at:half * I + at + m],
                                           xT[:, b.s, v * KT + k, 0:b.w], start=(j == 0), stop=(j == len(steps) - 1))
                    mm.then_inc(up_done, 1)

            def down(b):
                pe.wait_ge(dn_lo, b.n + 1)
                pe.wait_ge(a_lo, b.n * NC + NC)
                for t in range(b.bt):
                    wait(pe, y_ok, b.t_prev + min(t + 1, b.bt_prev))
                    steps = [(c, w, v) for c in range(NC) for w, v in ((0, 0), (1, 0), (0, 1))]
                    for j, (c, w, v) in enumerate(steps):
                        m = IC[c][1]
                        mm = pe.matmul(py[t][:], a_hl[0:m, b.s, v, c, t * P:(t + 1) * P], dn_hl[0:m, b.s, w, c, :],
                                       start=(j == 0), stop=(j == len(steps) - 1))
                    mm.then_inc(down_done, 1)

            def turn(cur, nxt, after):
                if nxt:
                    up(nxt)
                if after:
                    turn_x(after)
                down(cur)

            pe.wait_ge(route_const, 10)
            turn_x(blk(0))
            up(blk(0))
            turn_x(blk(1))
            pe.wait_ge(mask_ready, 1)
            flat = picked[:].rearrange("p t e -> p (t e)")
            pe.matmul(py[0][:, 0:NT * E], before[:], flat, start=True, stop=True)
            pe.matmul(py[1][:, 0:NT * E], ones[:], flat, start=True, stop=True).then_inc(rank_done, 1)
            pe.wait_ge(rank_read, 1)
            expert_turns(turn, pe.Fori)

        @block.vector
        def _(dve):
            steps = [0]

            def link(ins):
                steps[0] += 1
                ins.then_inc(chain, 1)
                dve.wait_ge(chain, steps[0])

            dve.memset(wshared[:], 1.0 / WS)
            dve.memset(xin[:, :, 0:TAPS - 1], 0.0).then_inc(dve_const, 1)
            dve.wait_ge(act_const, 1)
            dve.tensor_scalar(negA[:], alog[:], -1.0, None, ALU.mult).then_inc(dve_const, 1)
            dve.tensor_scalar(taps_half[:], taps[:], 0.5, None, ALU.mult)
            dve.tensor_scalar(cbias[:], cbias[:], 0.5, None, ALU.mult).then_inc(dve_const, 1)
            dve.wait_ge(ident_ok, 1)
            for e in range(ET):
                ins = dve.tensor_scalar(Ddiag[:, e, :], ident[:], Dcol[:, e:e + 1], None, ALU.mult)
            ins.then_inc(dve_const, 1)
            dve.wait_ge(dve_const, 4)

            def moments(n, tiles):
                for c in range(4):
                    ins = dve.bn_stats(stat[:, c, :], tiles(c))
                link(ins)
                for c in range(4):
                    ins = dve.bn_aggr(mv[:, c, :], stat[:, c, :])
                link(ins)
                dve.tensor_scalar(veps[:], mv[:, :, 1], EPS, None, ALU.add).then_inc(ln_var, 1)
                dve.wait_ge(ln_rstd, n + 1)
                link(dve.scalar_tensor_tensor(out=nmr[:], in0=mv[:, :, 0], scalar=-1.0, in1=rstd[:],
                                              op0=ALU.mult, op1=ALU.mult))

            def pre(b):
                n0 = max(0, 2 * b - 1)
                dve.wait_ge(x_in, 16 * (b + 1))
                moments(n0, lambda c: xs[:, b % 2, c, :])
                link(dve.tensor_scalar(rstd[:], rstd[:], 0.5, None, ALU.mult))
                link(dve.tensor_scalar(nmr[:], nmr[:], 0.5, None, ALU.mult))
                for e in range(ET):
                    n = 4 * b + e
                    dve.wait_ge(xin_ready, n + 1)
                    for k in range(TAPS - 1):
                        ins = dve.scalar_tensor_tensor(out=cv[:, e % 2, :], in0=xin[:, e % 2, k:k + L],
                                                       scalar=taps_half[:, e, k:k + 1], in1=cv[:, e % 2, :],
                                                       op0=ALU.mult, op1=ALU.add)
                        if k < TAPS - 2:
                            link(ins)
                    ins.then_inc(conv_done, 1)
                    dve.tensor_scalar(sz[:, b % 2, e, :], xs[:, b % 2, e, :], rstd[:, e:e + 1], nmr[:, e:e + 1],
                                      ALU.mult, ALU.add).then_inc(z_half, 1)
                    dve.wait_ge(tanh_u, n + 1)
                    dve.scalar_tensor_tensor(out=u[:, b % 2, e, :], in0=th[:, e % 2, :], scalar=1.0,
                                             in1=cv[:, e % 2, :], op0=ALU.add, op1=ALU.mult).then_inc(u_ready, 1)
                for e in range(ET):
                    n = 4 * b + e
                    dve.wait_ge(tanh_z, n + 1)
                    dve.scalar_tensor_tensor(out=sz[:, b % 2, e, :], in0=th[:, e % 2, :], scalar=1.0,
                                             in1=sz[:, b % 2, e, :], op0=ALU.add, op1=ALU.mult).then_inc(sz_ready, 1)

            def scan(b, e):
                first = (4 * b + e) * DS

                def recur(q, r, free=True):
                    dve.wait_ge(dA_ready, q * 4 + (first + r + 1))
                    if r % 2 == 0:
                        dve.wait_ge(dbu_ready, q * 2 + (first // 2 + r // 2 + 1))
                    if free:
                        dve.wait_ge(sum_done, q * 4 + (first + r - 3))
                    dve.tensor_tensor_scan(hc[:, r % 4, :], dA[r % 2][:], dBu[:, (r // 2) % 2, r % 2, :], 0.0,
                                           ALU.mult, ALU.add).then_inc(scan_done, 1)

                def weigh(q, r):
                    dve.wait_ge(scan_done, q * 4 + (first + r + 1))
                    dve.tensor_tensor(hc[:, r, :], hc[:, r, :], Cf[:, bass.ds(q * (4 * L) + r * L, L)],
                                      ALU.mult).then_inc(hc_ready, 1)

                def four(q, last=False):
                    if e == 0:
                        dve.wait_ge(c_ready, q * 16 + 16 * (4 * b + 1))
                    for r in range(4):
                        if not (last and r == 3):
                            recur(q, r + 1, free=first or r == 3 or not isinstance(q, int) or q > 0)
                        weigh(q, r)

                recur(0, 0, free=first > 0)
                if first == 0:
                    four(0)
                with dve.Fori(0 if first else 1, SG - 1) as q:
                    four(q)
                four(SG - 1, last=True)

            def gated(b, e):
                n = 4 * b + e
                dve.wait_ge(sum_done, DS * (n + 1))
                dve.wait_ge(sz_ready, n + 1)
                dve.tensor_tensor(yv[:, e, :], yp[:], sz[:, b % 2, e, :], ALU.mult).then_inc(yv_done, 1)

            def post(b):
                for c in range(LC):
                    t = LC * b + c
                    dve.wait_ge(yT_done, t + 1)
                    ins = dve.tensor_tensor(xs[:, b % 2, c, :], pp[c % 2][:], xs[:, b % 2, c, :], ALU.add)
                    ins.then_inc(x2_ready, 1)
                dve.wait_ge(x2_ready, LC * b + LC)
                moments(2 * b + 2 if b < NB - 1 else 2 * NB - 1, lambda c: xs[:, b % 2, c, :])
                for c in range(LC):
                    t = LC * b + c
                    if t >= 2:
                        dve.wait_ge(xnT_done, t - 1)
                    dve.tensor_scalar(xn[:, c % 2, :], xs[:, b % 2, c, :], rstd[:, c:c + 1], nmr[:, c:c + 1],
                                      ALU.mult, ALU.add).then_inc(xn_ready, 1)
                    dve.wait_ge(hi_ready, t + 1)
                    dve.tensor_copy(row[:, c % 2, RW - 2:RW].bitcast(I32), tokens[:, t:t + 1])
                    dve.tensor_copy(row[:, c % 2, RW - 4:RW - 2].bitcast(F32), wshared[:])
                    dve.tensor_tensor(row[:, c % 2, H:2 * H], xn[:, c % 2, :], row[:, c % 2, 0:H],
                                      ALU.subtract).then_inc(row_ready, 1)
                    dve.wait_ge(gate_done, t + 1)
                    dve.tensor_copy(logits[:, t, :], pq[:, 0:E]).then_inc(lg_copied, 1)

            pre(0)
            for b in range(NB):
                scan(b, 0)
                if b:
                    post(b - 1)
                gated(b, 0)
                scan(b, 1)
                gated(b, 1)
                if b + 1 < NB:
                    pre(b + 1)
                scan(b, 2)
                gated(b, 2)
                scan(b, 3)
                gated(b, 3)
            post(NB - 1)

            def lo_up(b, k):
                dve.wait_ge(up_hi, b.n * KT + (k + 1))
                wait(dve, up_done, b.n * NC - NC)
                dve.scalar_tensor_tensor(out=up_hl[:, b.s, 1, k, :], in0=up_raw[:, b.s, k, :], scalar=WS,
                                         in1=up_hl[:, b.s, 0, k, :], op0=ALU.mult,
                                         op1=ALU.subtract).then_inc(up_lo, 1)

            def lo_dn(b):
                dve.wait_ge(dn_hi, b.n + 1)
                m = IC[-1][1]
                dve.scalar_tensor_tensor(out=dn_hl[:, b.s, 1, 0:2, :], in0=dn_raw[:, b.s, 0:2, :], scalar=WS,
                                         in1=dn_hl[:, b.s, 0, 0:2, :], op0=ALU.mult, op1=ALU.subtract)
                dve.scalar_tensor_tensor(out=dn_hl[0:m, b.s, 1, 2, :], in0=dn_raw[0:m, b.s, 2, :], scalar=WS,
                                         in1=dn_hl[0:m, b.s, 0, 2, :], op0=ALU.mult,
                                         op1=ALU.subtract).then_inc(dn_lo, 1)

            def keep_meta(b):
                dve.wait_ge(rows_in[b.s], half_count(b.n, b.s, 16))
                dve.tensor_copy(meta[:, bass.ds(b.t, b.bt), :],
                                xb[:, b.s, 0:b.bt, RW - 4:RW].bitcast(U32)).then_inc(meta_ok, 1)

            def gate_up(b, c):
                dve.wait_ge(silu_ok, b.n * NC + (c + 1))
                wait(dve, a_lo, b.n * NC + (c + 1 - NC))
                m = IC[c][1]
                dve.scalar_tensor_tensor(out=a32[0:m, c, 0:b.w], in0=pu[c][0:m, TB:TB + b.w], scalar=1.0 / WS,
                                         in1=sg[0:m, c, 0:b.w], op0=ALU.mult, op1=ALU.mult).then_inc(a_ok, 1)

            def lo_a(b, c):
                dve.wait_ge(a_hi, b.n * NC + (c + 1))
                m = IC[c][1]
                dve.tensor_tensor(a_hl[0:m, b.s, 1, c, 0:b.w], a32[0:m, c, 0:b.w], a_hl[0:m, b.s, 0, c, 0:b.w],
                                  ALU.subtract).then_inc(a_lo, 1)

            def weigh_y(b):
                wait(dve, y_added, b.t_prev * 16)
                dve.tensor_copy(dest[:, b.s, 0:b.bt], meta[:, bass.ds(b.t, b.bt), 1])
                for t in range(b.bt):
                    dve.wait_ge(down_done, b.t + (t + 1))
                    dve.tensor_scalar(yb[:, b.s, t, :], py[t][:], meta[:, bass.ds(b.t + t, 1), 0].bitcast(F32),
                                      None, ALU.mult).then_inc(y_ok, 1)

            def turn(cur, nxt, after):
                if after:
                    keep_meta(after)
                if nxt:
                    lo_dn(nxt)
                    if after:
                        lo_up(after, 0)
                    for c in range(NC):
                        gate_up(nxt, c)
                        if after and c + 1 < KT:
                            lo_up(after, c + 1)
                        lo_a(nxt, c)
                weigh_y(cur)

            def rows3(ap, n):
                return ap.unsqueeze(2).to_broadcast([P, ap.shape[1], n])

            def cols3(ap, n):
                return ap.unsqueeze(1).to_broadcast([P, n, ap.shape[1]])

            for s in row_stored:
                dve.wait_ge(s, 16 * NT // 2)
            dve.wait_ge(x2_stored, 16 * NT)
            dve.wait_ge(lg_copied, NT)
            link(dve.tensor_reduce(r_max[:], logits[:], AX.X, ALU.max))
            dve.tensor_tensor(r_exp[:], logits[:], rows3(r_max[:], E), ALU.subtract).then_inc(shifted, 1)
            dve.memset(g_in[:], -1.0)
            for k in range(KT):
                lo_up(blk(0), k)
            lo_dn(blk(0))
            keep_meta(blk(0))
            dve.wait_ge(exp_ready, 1)
            link(dve.tensor_reduce(r_sum[:], r_exp[:], AX.X, ALU.add))
            link(dve.reciprocal(r_inv[:], r_sum[:]))
            link(dve.tensor_tensor(score[:], r_exp[:], rows3(r_inv[:], E), ALU.mult))
            link(dve.tensor_reduce(g_in[:, :, 0:G], score[:].rearrange("p t (g j) -> p t g j", g=G), AX.X, ALU.max))
            for t in range(NT):
                ins = dve.max(g_top[:, t, :], g_in[:, t, :])
            link(ins)
            for t in range(NT):
                ins = dve.max_index(g_idx[:, t, :], g_top[:, t, :], g_in[:, t, :])
            dve.wait_ge(route_const, 10)
            link(ins)
            link(dve.tensor_copy(g_idf[:], g_idx[:]))
            dve.tensor_tensor(g_mask[:], cols3(iota_e[:, 0:G], NT), g_idf[:, :, 0:1].to_broadcast([P, NT, G]),
                              ALU.is_equal)
            link(dve.tensor_tensor(g_mask2[:], cols3(iota_e[:, 0:G], NT), g_idf[:, :, 1:2].to_broadcast([P, NT, G]),
                                   ALU.is_equal))
            link(dve.tensor_tensor(g_mask[:], g_mask[:], g_mask2[:], ALU.add))
            link(dve.tensor_tensor(score[:].rearrange("p t (g j) -> p (t g) j", g=G),
                                   score[:].rearrange("p t (g j) -> p (t g) j", g=G),
                                   rows3(g_mask[:].rearrange("p t g -> p (t g)"), E // G), ALU.mult))
            for t in range(NT):
                ins = dve.max(e_top[:, t, :], score[:, t, :])
            link(ins)
            for t in range(NT):
                ins = dve.max_index(e_idx[:, t, :], e_top[:, t, :], score[:, t, :])
            link(ins)
            link(dve.tensor_copy(e_idf[:], e_idx[:]))
            for k in range(TOPK):
                ins = dve.tensor_tensor(onehot[:, k], cols3(iota_e[:], NT),
                                        e_idf[:, :, k:k + 1].to_broadcast([P, NT, E]), ALU.is_equal)
            link(ins)
            link(dve.tensor_tensor(picked[:], onehot[:, 0], onehot[:, 1], ALU.add))
            link(dve.tensor_tensor(picked[:], picked[:], onehot[:, 2], ALU.add))
            dve.tensor_tensor(picked[:], picked[:], onehot[:, 3], ALU.add).then_inc(mask_ready, 1)
            link(dve.tensor_reduce(r_sum[:], e_top[:, :, 0:TOPK], AX.X, ALU.add))
            link(dve.tensor_scalar(r_sum[:], r_sum[:], 1e-20, None, ALU.add))
            link(dve.reciprocal(r_inv[:], r_sum[:]))
            link(dve.tensor_tensor(w_top[:], e_top[:, :, 0:TOPK], rows3(r_inv[:], TOPK), ALU.mult))
            link(dve.tensor_scalar(w_top[:], w_top[:], 1.0 / WS, None, ALU.mult))
            dve.wait_ge(rank_done, 1)
            link(dve.tensor_copy(count[:], py[1][:, 0:NT * E].rearrange("p (t e) -> p e t", e=E)))
            flat = lambda a: a[:].rearrange("p e t -> p (e t)")
            link(dve.tensor_tensor_scan(flat(cum_t), flat(keep), flat(count), 0.0, ALU.mult, ALU.add))
            link(dve.tensor_tensor(over[:], cum_t[:, :, NT - 1:NT].to_broadcast([P, E, NT]), cols3(iota_m[:], E),
                                   ALU.is_gt))
            dve.tensor_reduce(big_e[:], over[:].rearrange("p e (m two) -> p e m two", two=2)[:, :, :, 1], AX.X, ALU.add)
            link(dve.tensor_reduce(tiles_e[:], over[:], AX.X, ALU.add))
            link(dve.tensor_tensor_scan(big_to[:], ones[:, 0:E], big_e[:], 0.0, ALU.mult, ALU.add))
            link(dve.tensor_tensor(big_from[:], big_to[:], big_e[:], ALU.subtract))
            dve.tensor_scalar(big_to[:], big_to[:], float(NBIG), None, ALU.min)
            link(dve.tensor_scalar(big_from[:], big_from[:], float(NBIG), None, ALU.min))
            link(dve.tensor_tensor(big_e[:], big_to[:], big_from[:], ALU.subtract))
            link(dve.scalar_tensor_tensor(out=small_e[:], in0=big_e[:], scalar=-2.0, in1=tiles_e[:],
                                          op0=ALU.mult, op1=ALU.add))
            link(dve.tensor_tensor_scan(small_to[:], ones[:, 0:E], small_e[:], 0.0, ALU.mult, ALU.add))
            dve.tensor_tensor(below[:, 0:NBIG], cols3(big_to[:], NBIG), rows3(iota_b[:, 0:NBIG], E), ALU.is_le)
            link(dve.tensor_tensor(below[:, NBIG:], cols3(small_to[:], NSMALL), rows3(iota_b[:, 0:NSMALL], E), ALU.is_le))
            link(dve.tensor_reduce(bexpf[:], below[:], AX.X, ALU.add))
            dve.tensor_scalar(bexp[:], bexpf[:], float(E - 1), None, ALU.min).then_inc(experts_ready, 1)
            dve.tensor_scalar(in_big[:], big_e[:], float(TB), None, ALU.mult)
            dve.tensor_scalar(big_from[:], big_from[:], float(TB), None, ALU.mult)
            link(dve.tensor_tensor(small_to[:], small_to[:], small_e[:], ALU.subtract))
            link(dve.tensor_scalar(to_small[:], small_to[:], float(P), float(NBIG * TB), ALU.mult, ALU.add))
            link(dve.tensor_tensor(to_small[:], to_small[:], in_big[:], ALU.subtract))
            link(dve.tensor_tensor(to_small[:], to_small[:], big_from[:], ALU.subtract))
            link(dve.tensor_tensor(cum_t[:], cum_t[:], count[:], ALU.subtract))
            dve.tensor_tensor(rank[:], py[0][:, 0:NT * E].rearrange("p (t e) -> p t e", e=E),
                              cum_t[:].rearrange("p e t -> p t e"), ALU.add).then_inc(rank_read, 1)
            dve.wait_ge(rank_read, 1)
            link(dve.tensor_tensor(place[:], rank[:], cols3(in_big[:], NT), ALU.is_ge))
            link(dve.tensor_tensor(place[:], place[:], cols3(to_small[:], NT), ALU.mult))
            link(dve.tensor_tensor(place[:], place[:], rank[:], ALU.add))
            link(dve.tensor_tensor(place[:], place[:], cols3(big_from[:], NT), ALU.add))
            for k in range(TOPK):
                link(dve.tensor_tensor(prod[:], onehot[:, k], place[:], ALU.mult))
                link(dve.tensor_reduce(slotf[:, k, :], prod[:], AX.X, ALU.add))
            dve.tensor_copy(slot[:], slotf[:]).then_inc(slot_ok, 1)

            for k in range(KT):
                lo_up(blk(1), k)
            keep_meta(blk(1))
            for c in range(NC):
                gate_up(blk(0), c)
                lo_a(blk(0), c)
            expert_turns(turn, dve.Fori)

def kernel(**inputs):
    import numpy as np
    import concourse.bacc as bacc
    from concourse.bass_utils import run_bass_kernel_spmd

    def tiles(a):
        return np.ascontiguousarray(a.reshape((-1, 128) + a.shape[1:]).swapaxes(0, 1))

    up = np.concatenate([inputs["L0_ffn_expert_up_w"],
                         inputs["L0_ffn_shared_up_w"].reshape(2, 2, 352, 512).swapaxes(0, 1).reshape(2, 704, 512)])
    down = np.concatenate([inputs["L0_ffn_expert_down_w"],
                           inputs["L0_ffn_shared_down_w"].reshape(512, 2, 352).swapaxes(0, 1)])
    upT = up.transpose(0, 2, 1).reshape(18, 4, 128, 704).transpose(0, 2, 1, 3)
    downT = down.transpose(0, 2, 1)
    arrays = {
        "x": inputs["x"].reshape(4, 4, 128, 512).transpose(0, 2, 1, 3),
        "ctxT": inputs["ctx_1024"].transpose(0, 2, 1).reshape(4, 2, 128, 512).transpose(0, 2, 1, 3),
        "in_projT": tiles(inputs["L0_xattn_in_proj_w"].T),
        "conv_w": tiles(inputs["L0_xattn_conv_w"]),
        "conv_b": tiles(inputs["L0_xattn_conv_b"]),
        "x_projT": tiles(inputs["L0_xattn_x_proj_w"].T),
        "dt_projT": inputs["L0_xattn_dt_proj_w"].T,
        "dt_b": tiles(inputs["L0_xattn_dt_proj_b"]),
        "A_log": tiles(inputs["L0_xattn_A_log"]).reshape(128, 64),
        "D": tiles(inputs["L0_xattn_D"]),
        "gateT": tiles(inputs["L0_ffn_gate_w"].T),
        "upT": upT,
        "downA": downT[:, :256].reshape(18, 2, 128, 512).transpose(0, 2, 1, 3),
        "downB": downT[:, 256:],
    }
    nc = bacc.Bacc("TRN2", target_bir_lowering=False, num_devices=1)
    feed, args = {}, []
    for name, a in arrays.items():
        a = np.ascontiguousarray(a)
        feed[f"in_{name}"] = a
        args.append(nc.dram_tensor(f"in_{name}", a.shape, mybir.dt.from_np(a.dtype), kind="ExternalInput").ap())
    args.append(nc.dram_tensor("out_0", (2048 + 128, 512), F32, kind="ExternalOutput").ap())
    build(nc, *args)
    got = run_bass_kernel_spmd(nc, [feed], core_ids=[0])
    return got.results[0]["out_0"][:2048].reshape(4, 512, 512)
```

```python
from contextlib import ExitStack

import concourse.bass as bass
from concourse import mybir

F32 = mybir.dt.float32
F16 = mybir.dt.float16
BF16 = mybir.dt.bfloat16
U32 = mybir.dt.uint32
I32 = mybir.dt.int32
ALU = mybir.AluOpType
ACT = mybir.ActivationFunctionType
AX = mybir.AxisListType

P = 128
NB = 4
L = 512
DM = 256
H = 512
DS = 16
DR = 16
TAPS = 4
ET = H // P
LC = L // P
T = NB * L
NT = T // P
E = 16
G = 4
EPS = 1e-5
SG = DS // 4
KT = H // P
I = 352
TOPK = 4
NS = 2
TB = 256
BT = TB // P
NSB = NS * T // TB
MAXT = (T * TOPK + E * (P - 1)) // P
NBIG = (MAXT - E) // 2
NSMALL = max(E, MAXT - 2 * NBIG)
NRB = NBIG + NSMALL
NA = NSB + NBIG - NSMALL
NBLK = NSB + NRB
TILES = 2 * NA + 3 * NSMALL
RW = 2 * H + 4
assert NS == 2 and NA % 2 == 0 and NSB % 2 == 0
SLOTS_AT = 4
RANK_AT = 2
PEELED = SLOTS_AT + 2
WS = 64.0
IC = [(c * P, min(P, I - c * P)) for c in range(-(-I // P))]
NC = len(IC)


class Blk:

    def __init__(self, n, s, bt, t, bt_prev, m, wn, new_w):
        self.n, self.s, self.bt, self.t, self.bt_prev, self.m = n, s, bt, t, bt_prev, m
        self.wn, self.new_w = wn, new_w
        self.t_prev = t - bt_prev
        self.w = bt * P


def blk(n):
    wn = n % NS if n < NSB else n - (NSB - NS)
    new_w = n < NS or n >= NSB
    if n < NA:
        return Blk(n, n % 2, BT, BT * n, BT, BT * n, wn, new_w)
    j, k = divmod(n - NA, 2)
    return Blk(n, k, BT - k, BT * NA + 3 * j + BT * k, BT - 1 if j and k == 0 else BT,
               BT * (NSB + NBIG) + j if k else BT * (NA + j), wn, new_w)


def blk_s(i, k):
    return Blk(i * 2 + k, k % 2, BT, i * (2 * BT) + BT * k, BT, i * (2 * BT) + BT * k, k % 2, False)


def blk_a(i, k):
    return Blk(i * 2 + k, k % 2, BT, i * (2 * BT) + BT * k, BT, i * (2 * BT) + BT * k, i * 2 + (k - NSB + NS), True)


def blk_b(j, k):
    t = BT * NA + 3 * (k // 2) + BT * (k % 2)
    m = j + (BT * (NSB + NBIG) + k // 2) if k % 2 else j * BT + BT * (NA + k // 2)
    return Blk(j * 2 + (NA + k), k % 2, BT - k % 2, j * 3 + t, BT - (1 - k % 2), m, j * 2 + (NA + k - NSB + NS), True)


def build(nc, x, ctxT, in_projT, conv_w, conv_b, x_projT, dt_projT, dt_b, A_log, D, gateT, upT, downA, downB, out):
    bc_dram = nc.dram_tensor("bc_dram", (NB, 2 * DS, L), F32, kind="Internal").ap()
    rows_dram = nc.dram_tensor("rows_dram", (T, RW // 2), U32, kind="Internal").ap()
    slots_dram = nc.dram_tensor("slots_dram", (MAXT * P, RW // 2), U32, kind="Internal").ap()

    with ExitStack() as ctx:
        def sb(name, shape, dt=F32):
            return ctx.enter_context(nc.sbuf_tensor(name, shape, dt))

        def pb(name):
            return ctx.enter_context(nc.psum_tensor(name, [P, 512], F32))

        def sem(name):
            return ctx.enter_context(nc.semaphore(name))

        ident = sb("ident", [P, P])
        inp_w = sb("inp_w", [P, DM // P, H])
        xp_w = sb("xp_w", [P, ET, DR + 2 * DS])
        dt_w = sb("dt_w", [DR, H])
        taps = sb("taps", [P, ET * TAPS])
        cbias = sb("cbias", [P, ET])
        dtbias = sb("dtbias", [P, ET])
        alog = sb("alog", [P, ET * DS])
        negA = sb("negA", [P, ET * DS])
        Dcol = sb("Dcol", [P, ET])
        Ddiag = sb("Ddiag", [P, ET, P])
        gate_w = sb("gate_w", [P, H // P, E])
        powexp = sb("powexp", [P, 4])
        logits = sb("logits", [P, NT, E])
        wshared = sb("wshared", [P, 1])
        tokens = sb("tokens", [P, NT], I32)
        pad_row = sb("pad_row", [P, 2, RW], F16)

        scan_mem = ExitStack()

        def sb(name, shape, dt=F32):
            return scan_mem.enter_context(nc.sbuf_tensor(name, shape, dt))

        def pb(name):
            return scan_mem.enter_context(nc.psum_tensor(name, [P, 512], F32))

        Bb = sb("Bb", [P, DS, L])
        Cb = sb("Cb", [P, DS, L])
        Cf = Cb[:].rearrange("p n l -> p (n l)")
        dBu = sb("dBu", [P, 2, 2, L])
        hc = sb("hc", [P, 4, L])
        delta = sb("delta", [P, 2, ET, L])
        u = sb("u", [P, 2, ET, L])
        du = sb("du", [P, 2, ET, L])
        xs = sb("xs", [P, 2, LC, H])
        ctxs = sb("ctxs", [P, DM // P, L])
        sz = sb("sz", [P, 2, ET, L])
        xin = sb("xin", [P, 2, L + TAPS - 1])
        xdbl = sb("xdbl", [DR + 2 * DS, L])
        yv = sb("yv", [P, ET, L])
        xn = sb("xn", [P, 2, H])
        xnT = sb("xnT", [P, 2, H])
        row = sb("row", [P, 2, RW], F16)
        stat = sb("stat", [P, 4, 6])
        mv = sb("mv", [P, 4, 2])
        veps = sb("veps", [P, 4])
        rstd = sb("rstd", [P, 4])
        nmr = sb("nmr", [P, 4])

        dA = [pb(f"dA{i}") for i in range(4)]
        yp = [pb(f"yp{i}") for i in range(2)]
        pp = [pb(f"pp{i}") for i in range(2)]
        scan_mem.close()

        def sb(name, shape, dt=F32):
            return ctx.enter_context(nc.sbuf_tensor(name, shape, dt))

        up_raw = sb("up_raw", [P, 2, KT, 2 * I])
        dn_raw = sb("dn_raw", [P, 2, NC, H])
        up_hl = sb("up_hl", [P, 2, 2, KT, 2 * I], F16)
        dn_hl = sb("dn_hl", [P, 2, 2, NC, H], F16)
        xT = sb("xT", [P, 2, 2 * KT, TB], F16)
        sg = sb("sg", [P, NC, TB])
        a32 = sb("a32", [P, NC, TB])
        a_hl = sb("a_hl", [P, 2, 2, NC, TB], F16)
        yb = sb("yb", [P, 2, BT, H])
        meta = sb("meta", [P, TILES, 2], U32)
        dest = sb("dest", [P, 2, BT], U32)
        r_max = sb("r_max", [P, NT])
        r_exp = sb("r_exp", [P, NT, E])
        r_sum = sb("r_sum", [P, NT])
        r_inv = sb("r_inv", [P, NT])
        score = sb("score", [P, NT, E])
        g_in = sb("g_in", [P, NT, 8])
        g_top = sb("g_top", [P, NT, 8])
        g_idx = sb("g_idx", [P, NT, 8], U32)
        g_idf = sb("g_idf", [P, NT, 8])
        g_mask = sb("g_mask", [P, NT, G])
        g_mask2 = sb("g_mask2", [P, NT, G])
        e_top = sb("e_top", [P, NT, 8])
        e_idx = sb("e_idx", [P, NT, 8], U32)
        e_idf = sb("e_idf", [P, NT, 8])
        w_top = sb("w_top", [P, NT, TOPK])
        onehot = sb("onehot", [P, TOPK, NT, E])
        picked = sb("picked", [P, NT, E])
        count = sb("count", [P, E, NT])
        cum_t = sb("cum_t", [P, E, NT])
        over = sb("over", [P, E, NT])
        tiles_e = sb("tiles_e", [P, E])
        big_e = sb("big_e", [P, E])
        big_to = sb("big_to", [P, E])
        big_from = sb("big_from", [P, E])
        small_e = sb("small_e", [P, E])
        small_to = sb("small_to", [P, E])
        in_big = sb("in_big", [P, E])
        to_small = sb("to_small", [P, E])
        rank = sb("rank", [P, NT, E])
        place = sb("place", [P, NT, E])
        prod = sb("prod", [P, NT, E])
        slotf = sb("slotf", [P, TOPK, NT])
        slot = sb("slot", [P, TOPK, NT], U32)
        below = sb("below", [P, NRB, E])
        bexpf = sb("bexpf", [P, NRB])
        bexp = sb("bexp", [P, NRB], I32)
        iota_e = sb("iota_e", [P, E])
        iota_m = sb("iota_m", [P, NT])
        iota_b = sb("iota_b", [P, NRB])
        keep = sb("keep", [P, E, NT])
        ones = sb("ones", [P, P])
        before = sb("before", [P, P])
        xr = sb("xr", [P, NT, RW], F16)

        def pb(name, shape=(P, 512), dt=F32):
            return ctx.enter_context(nc.psum_tensor(name, list(shape), dt))

        pr = pb("pr")
        pu = [pb(f"pu{i}") for i in range(NC)]
        spare = pb("spare")
        py = [pb(f"py{i}") for i in range(BT)]

        inp_in = sem("inp_in")
        w_in = sem("w_in")
        ctx_in = sem("ctx_in")
        x_in = sem("x_in")
        ident_ok = sem("ident_ok")
        pool_const = sem("pool_const")
        act_const = sem("act_const")
        dve_const = sem("dve_const")
        chain = sem("chain")
        inproj_done = sem("inproj_done")
        xin_ready = sem("xin_ready")
        conv_tap = sem("conv_tap")
        conv_done = sem("conv_done")
        u_ready = sem("u_ready")
        u_first = sem("u_first")
        xproj_done = sem("xproj_done")
        xdbl_ready = sem("xdbl_ready")
        bc_stored = sem("bc_stored")
        b_ready = sem("b_ready")
        c_ready = sem("c_ready")
        dt_done = sem("dt_done")
        dt_read = sem("dt_read")
        dt_exp = sem("dt_exp")
        dt_log = sem("dt_log")
        delta_ready = sem("delta_ready")
        du_ready = sem("du_ready")
        ln_var = sem("ln_var")
        ln_rstd = sem("ln_rstd")
        ln_shift = sem("ln_shift")
        norm_ok = sem("norm_ok")
        sz_ready = sem("sz_ready")
        dA_ready = sem("dA_ready")
        dbu_ready = sem("dbu_ready")
        scan_done = sem("scan_done")
        hc_ready = sem("hc_ready")
        sum_done = sem("sum_done")
        yv_done = sem("yv_done")
        yT_done = sem("yT_done")
        x2_ready = sem("x2_ready")
        xn_ready = sem("xn_ready")
        hi_ready = sem("hi_ready")
        row_ready = sem("row_ready")
        xnT_done = sem("xnT_done")
        xnT_copied = sem("xnT_copied")
        gate_done = sem("gate_done")
        lg_copied = sem("lg_copied")
        x2_stored = sem("x2_stored")
        row_stored = [sem(f"row_stored{i}") for i in range(2)]


        pad_ok = sem("pad_ok")
        pad_stored = sem("pad_stored")
        route_const = sem("route_const")
        shifted = sem("shifted")
        exp_ready = sem("exp_ready")
        mask_ready = sem("mask_ready")
        rank_done = sem("rank_done")
        rank_read = sem("rank_read")
        experts_ready = sem("experts_ready")
        xr_in = sem("xr_in")
        slot_ok = sem("slot_ok")
        xr_weight = sem("xr_weight")
        scattered = sem("scattered")
        up_in = [sem(f"up_in{i}") for i in range(2)]
        dn_in = [sem(f"dn_in{i}") for i in range(2)]
        xT_in = [sem(f"xT_in{i}") for i in range(2)]
        x_turns = sem("x_turns")
        meta_in = sem("meta_in")
        up_hi = sem("up_hi")
        up_lo = sem("up_lo")
        dn_hi = sem("dn_hi")
        dn_lo = sem("dn_lo")
        meta_ok = sem("meta_ok")
        up_done = sem("up_done")
        silu_ok = sem("silu_ok")
        a_ok = sem("a_ok")
        a_hi = sem("a_hi")
        a_lo = sem("a_lo")
        down_done = sem("down_done")
        y_ok = sem("y_ok")
        y_added = sem("y_added")
        add_turns = sem("add_turns")

        ROWS_STORED = (16 * (NT - LC // 2), 16 * (LC // 2))

        def scan_over(eng):
            eng.wait_ge(dbu_ready, 8 * NB * ET)
            eng.wait_ge(scan_done, 16 * NB * ET)
            eng.wait_ge(hc_ready, 16 * NB * ET)
            eng.wait_ge(sum_done, 16 * NB * ET)
            eng.wait_ge(yv_done, NB * ET)

        def wait(eng, s, v):
            if not isinstance(v, int) or v > 0:
                eng.wait_ge(s, v)

        def half_count(n, s, step):
            if isinstance(n, int):
                return step * (n // 2 + 1)
            return n * (step // 2) + (step - s * (step // 2))

        def quads(fori, four, straight=False):
            if straight:
                for q in range(SG):
                    four(q)
                return
            four(0)
            with fori(1, SG - 1) as q:
                four(q)
            four(SG - 1)

        def first(q):
            return isinstance(q, int) and q == 0

        def last(q):
            return isinstance(q, int) and q == SG - 1

        def part(buf, b, e):
            return buf[:].rearrange("p b e l -> p (b e l)")[:, bass.ds(e * L + (b % 2) * (ET * L), L)]

        def expert_turns(turn, fori, before_routed=None):
            def at(n):
                return blk(n) if n < NBLK else None

            def peeled(lo, hi):
                for n in range(lo, hi):
                    turn(at(n), at(n + 1), at(n + 2))

            peeled(0, PEELED)
            with fori(PEELED // 2, NSB // 2 - 1) as i:
                for k in range(2):
                    turn(blk_s(i, k), blk_s(i, k + 1), blk_s(i, k + 2))
            peeled(NSB - 2, NSB)
            if before_routed:
                before_routed()
            with fori(NSB // 2, NA // 2 - 1) as i:
                for k in range(2):
                    turn(blk_a(i, k), blk_a(i, k + 1), blk_a(i, k + 2))
            peeled(NA - 2, NA + 2)
            with fori(1, NSMALL - 1) as j:
                for k in range(2):
                    turn(blk_b(j, k), blk_b(j, k + 1), blk_b(j, k + 2))
            peeled(NBLK - 2, NBLK)

        block = ctx.enter_context(nc.Block())

        @block.sync
        def _(sp):
            sp.dma_start(inp_w[:], in_projT).then_inc(inp_in, 16)
            for dst, src in ((xp_w[:], x_projT), (dt_w[:], dt_projT), (taps[:], conv_w),
                             (cbias[:], conv_b), (dtbias[:], dt_b), (alog[:], A_log), (Dcol[:], D),
                             (gate_w[:], gateT)):
                sp.dma_start(dst, src).then_inc(w_in, 16)
            def broadcast(b):
                sp.wait_ge(bc_stored, 16 * (b + 1))
                for q in range(SG):
                    if b:
                        sp.wait_ge(dbu_ready, 8 * (4 * b - 1) + 2 * q + 2)
                    sp.dma_start(Bb[:, 4 * q:4 * q + 4, :],
                                 bc_dram[b, 4 * q:4 * q + 4, :].partition_broadcast(P)).then_inc(b_ready, 16)
                    if b:
                        sp.wait_ge(hc_ready, 16 * (4 * b - 1) + 4 * q + 4)
                    sp.dma_start(Cb[:, 4 * q:4 * q + 4, :],
                                 bc_dram[b, DS + 4 * q:DS + 4 * q + 4, :].partition_broadcast(P)).then_inc(c_ready, 16)
                    sp.wait_ge(b_ready, 16 * (4 * b + q + 1))
                    sp.wait_ge(c_ready, 16 * (4 * b + q + 1))

            def store_bc(b):
                sp.wait_ge(xdbl_ready, b + 1)
                sp.dma_start(bc_dram[b], xdbl[DR:, :]).then_inc(bc_stored, 16)

            def store_x2(b):
                for c in range(LC):
                    t = LC * b + c
                    sp.wait_ge(x2_ready, t + 1)
                    sp.dma_start(out[t * P:(t + 1) * P, :], xs[:, b % 2, c, :]).then_inc(x2_stored, 16)

            def store_row(t, s):
                sp.wait_ge(row_ready, t + 1)
                sp.dma_start(rows_dram[t * P:(t + 1) * P, :], row[:, s, :].bitcast(U32)).then_inc(row_stored[s], 16)

            store_bc(0)
            sp.dma_start(ctxs[:], ctxT[1]).then_inc(ctx_in, 16)
            broadcast(0)
            sp.dma_start(xs[:, 1], x[1]).then_inc(x_in, 16)
            sp.wait_ge(pad_ok, 3)
            for s in range(2):
                tiles = slots_dram.rearrange("(n p) c -> p n c", p=P)[:, s::2, :]
                sp.dma_start(tiles, pad_row[:, s, :].bitcast(U32).unsqueeze(1).to_broadcast(
                    [P, tiles.shape[1], RW // 2])).then_inc(pad_stored, 16)
            sp.dma_start(out[T:, :].rearrange("(s p) c -> p s c", p=P),
                         pad_row[:, :, 0:2 * H].bitcast(F32)).then_inc(pad_stored, 16)
            for b in range(NB):
                if b:
                    store_x2(b - 1)
                if b + 1 < NB:
                    store_bc(b + 1)
                if b:
                    for c in range(LC):
                        store_row(LC * (b - 1) + c, 0)
                if b + 1 < NB:
                    if b + 2 < NB:
                        sp.wait_ge(inproj_done, 4 * (b + 2))
                        sp.dma_start(ctxs[:], ctxT[b + 2]).then_inc(ctx_in, 16)
                    if b:
                        sp.wait_ge(x2_stored, 16 * 4 * b)
                        sp.wait_ge(xn_ready, 4 * b)
                        sp.dma_start(xs[:, (b + 1) % 2], x[b + 1]).then_inc(x_in, 16)
                    broadcast(b + 1)
            def load_up(b, e):
                wait(sp, up_lo, b.wn * KT - KT)
                sp.dma_start(up_raw[:, b.s], upT[bass.ds(e, 1)].squeeze(0)).then_inc(up_in[b.s], 16)

            def load_dn(b, e):
                wait(sp, dn_lo, b.wn - 1)
                sp.dma_start(dn_raw[:, b.s, 0:2, :], downA[bass.ds(e, 1)].squeeze(0)).then_inc(dn_in[b.s], 16)
                sp.dma_start(dn_raw[0:IC[-1][1], b.s, 2, :], downB[bass.ds(e, 1)].squeeze(0)).then_inc(dn_in[b.s], 16)

            def load_xT(b, src):
                wait(sp, up_done, b.n * NC - NC)
                sp.sem_inc(x_turns, 1)
                sp.dma_start_transpose(xT[:, b.s, :, 0:b.w], src.bitcast(F16)[:, 0:2 * H]).then_inc(xT_in[b.s], 16)

            scan_over(sp)
            load_up(blk(0), E)
            store_x2(NB - 1)
            sp.wait_ge(row_stored[0], 16 * LC)
            load_xT(blk(0), rows_dram[0:TB, :])
            load_dn(blk(0), E)
            for c in range(LC):
                store_row(LC * (NB - 1) + c, c % 2)
            load_up(blk(1), E + 1)
            load_xT(blk(1), rows_dram[0:TB, :])
            load_dn(blk(1), E + 1)
            def shared(i, blocks):
                for b in blocks:
                    load_xT(b, rows_dram[bass.ds(i * TB, TB), :])

            shared(1, (blk(2), blk(3)))
            sp.wait_ge(lg_copied, NB)
            for s in range(2):
                sp.wait_ge(row_stored[s], ROWS_STORED[s])
            sp.wait_ge(x2_stored, 16 * NT)
            sp.dma_start(xr[:].bitcast(U32), rows_dram.rearrange("(t p) c -> p t c", p=P)).then_inc(xr_in, 16)
            with sp.Fori(2, NSB // 2) as i:
                shared(i, (blk_s(i, 0), blk_s(i, 1)))
            sp.wait_ge(experts_ready, 1)

            def routed(b, at, row):
                e = sp.value_load(bexp[0:1, bass.ds(at, 1)], min_val=0, max_val=E - 1)
                load_up(b, e)
                load_dn(b, e)
                load_xT(b, slots_dram[bass.ds(row, b.w), :])

            sp.wait_ge(scattered, 16 * TOPK * NT)
            sp.dma_start(meta[:, BT * NSB:, :],
                         slots_dram[:, H:].rearrange("(t p) c -> p t c", p=P)).then_inc(meta_in, 16)
            with sp.Fori(0, (NA - NSB) // 2) as i:
                for s in range(2):
                    routed(blk_a(i, NSB + s), i * 2 + s, i * (2 * TB) + s * TB)

            def big_small(j, big, small):
                routed(big, j + (NA - NSB), j * TB + (NA - NSB) * TB)
                routed(small, j + NBIG, j * P + NBIG * TB)

            big_small(0, blk(NA), blk(NA + 1))
            with sp.Fori(1, NSMALL) as j:
                big_small(j, blk_b(j, 0), blk_b(j, 1))

        @block.gpsimd
        def _(pool):
            pool.memset(ident[:], 0.0).then_inc(pool_const, 1)
            pool.memset(powexp[:], -0.5).then_inc(pool_const, 1)
            pool.wait_ge(pool_const, 2)
            pool.affine_select(out=ident[:], in_=ident[:], compare_op=ALU.not_equal, fill=1.0, base=0,
                               pattern=[[-1, P]], channel_multiplier=1).then_inc(ident_ok, 1)

            pool.memset(pad_row[:, :, 0:RW - 2], 0.0).then_inc(pad_ok, 1)
            pool.iota(pad_row[:, :, RW - 2:RW].bitcast(I32), [[P, 2], [0, 1]], base=T,
                      channel_multiplier=1).then_inc(pad_ok, 1)
            pool.iota(tokens[:], [[P, NT]], base=0, channel_multiplier=1).then_inc(pad_ok, 1)

            def power(n):
                pool.wait_ge(ln_var, n + 1)
                pool.tensor_tensor(rstd[:], veps[:], powexp[:], ALU.pow).then_inc(ln_rstd, 1)

            def step_size(b, e):
                pool.wait_ge(dt_log, 1 if b == 0 and first(e) else b + 2)
                pool.tensor_tensor(part(delta, b, e), part(delta, b, e), part(du, b, e), ALU.add).then_inc(delta_ready, 1)
                pool.wait_ge(delta_ready, e + (4 * b + 1))
                pool.tensor_tensor(part(du, b, e), part(delta, b, e), part(u, b, e), ALU.mult).then_inc(du_ready, 1)

            def scan(b, e):
                pool.wait_ge(du_ready, 4 * b + e + 1)
                start = (4 * b + e) * 8

                def four(q):
                    if e == 0:
                        pool.wait_ge(b_ready, q * 16 + 16 * (4 * b + 1))
                    for s in range(2):
                        if start or not first(q):
                            pool.wait_ge(scan_done, q * 4 + (2 * (start + s) - 2))
                        src = du[:, b % 2, e, :].unsqueeze(1).to_broadcast([P, 2, L])
                        pool.tensor_tensor(dBu[:, s, :, :], src, Bb[:, bass.ds(q * 4 + 2 * s, 2), :],
                                           ALU.mult).then_inc(dbu_ready, 1)
                    if e == 0 and b and not last(q):
                        step_size(b, q + 1)
                    if e == 0 and b == 0 and not first(q):
                        step_size(0, q)
                    if e == 1 and b and first(q):
                        power(2 * b)
                    if e == 3 and b + 1 < NB:
                        if first(q):
                            power(2 * b + 1)
                        if q == 2:
                            step_size(b + 1, 0)

                quads(pool.Fori, four, straight=e == 3 and b + 1 < NB)

            power(0)
            step_size(0, 0)
            for b in range(NB):
                for e in range(ET):
                    scan(b, e)
            power(2 * NB - 1)
            scan_over(pool)
            pool.memset(meta[:, 0:BT * NSB, 0].bitcast(F32), 1.0 / WS).then_inc(meta_ok, 1)
            pool.iota(meta[:, 0:BT * NSB, 1].bitcast(I32), [[TB, NSB // 2], [0, NS], [P, BT]], base=0,
                      channel_multiplier=1).then_inc(meta_ok, 1)

            pool.iota(iota_e[:], [[1, E]], base=0, channel_multiplier=0,
                      allow_small_or_imprecise_dtypes=True).then_inc(route_const, 1)
            pool.iota(iota_m[:], [[P, NT]], base=0, channel_multiplier=0,
                      allow_small_or_imprecise_dtypes=True).then_inc(route_const, 1)
            pool.iota(iota_b[:], [[1, NRB]], base=0, channel_multiplier=0,
                      allow_small_or_imprecise_dtypes=True).then_inc(route_const, 1)
            pool.memset(ones[:], 1.0).then_inc(route_const, 1)
            pool.memset(before[:], 1.0).then_inc(route_const, 1)
            pool.memset(keep[:, :, 1:], 1.0).then_inc(route_const, 1)
            pool.memset(keep[:, :, 0:1], 0.0).then_inc(route_const, 1)
            pool.wait_ge(route_const, 7)
            pool.affine_select(out=before[:], in_=before[:], compare_op=ALU.is_gt, fill=0.0, base=0,
                               pattern=[[1, P]], channel_multiplier=-1).then_inc(route_const, 1)

            def scatter(k, tiles):
                for t in tiles:
                    pool.indirect_dma_start(out=slots_dram[:, :],
                                            out_offset=bass.IndirectOffsetOnAxis(ap=slot[:, k, t:t + 1], axis=0),
                                            in_=xr[:, t, :].bitcast(U32), in_offset=None).then_inc(scattered, 16)

            def add(b):
                for t in range(b.bt):
                    if t == 0:
                        wait(pool, y_added, b.t * 16)
                    pool.wait_ge(y_ok, b.t + (t + 1))
                    pool.sem_inc(add_turns, 1)
                    pool.indirect_dma_start(out=out[:, :],
                                            out_offset=bass.IndirectOffsetOnAxis(ap=dest[:, b.s, t:t + 1], axis=0),
                                            in_=yb[:, b.s, t, :], in_offset=None,
                                            compute_op=ALU.add).then_inc(y_added, 16)

            for n in range(SLOTS_AT):
                add(blk(n))
            pool.wait_ge(pad_stored, 48)
            pool.wait_ge(xr_in, 16)
            pool.wait_ge(slot_ok, 1)
            for h in range(2 * TOPK):
                k = h // 2
                if h % 2 == 0:
                    if k:
                        pool.wait_ge(scattered, 16 * NT * k)
                    pool.tensor_copy(xr[:, :, RW - 4:RW - 2].bitcast(F32), w_top[:, :, k:k + 1]).then_inc(xr_weight, 1)
                    pool.wait_ge(xr_weight, k + 1)
                scatter(k, range(NT // 2 * (h % 2), NT // 2 * (h % 2 + 1)))
                add(blk(SLOTS_AT + h))
            with pool.Fori(TOPK + SLOTS_AT // 2, NA // 2) as i:
                for k in range(2):
                    add(blk_a(i, k))
            for n in range(NA, NA + 2):
                add(blk(n))
            with pool.Fori(1, NSMALL) as j:
                for k in range(2):
                    add(blk_b(j, k))
            pool.wait_ge(y_added, 16 * TILES)

        @block.scalar
        def _(act):
            act.dma_start(ctxs[:], ctxT[0]).then_inc(ctx_in, 16)
            act.dma_start(xs[:, 0], x[0]).then_inc(x_in, 16)
            act.wait_ge(w_in, 16 * 8)
            act.activation(alog[:], alog[:], ACT.Exp).then_inc(act_const, 1)


            def conv_in(b, e, d):
                n = e + 4 * b
                s = e % 2 if d == 2 else 0
                act.wait_ge(inproj_done, n + 1)
                wait(act, conv_done, n + 1 - d)
                act.activation(xin[:, s, TAPS - 1:], pp[s][:], ACT.Copy)
                act.activation(part(u, b, e), pp[s][:], ACT.Identity, bias=cbias[:, bass.ds(e, 1)],
                               scale=taps[:, bass.ds(e * TAPS + (TAPS - 1), 1)]).then_inc(xin_ready, 1)

            def silu_u(b):
                act.wait_ge(conv_done, 4 * b + 4)
                act.activation(u[:, b % 2], u[:, b % 2], ACT.Silu).then_inc(u_ready, 1)

            def silu_first(e):
                act.wait_ge(conv_done, e + 1)
                act.activation(u[:, 0, e], u[:, 0, e], ACT.Silu).then_inc(u_ready if e == ET - 1 else u_first, 1)

            def silu_z(b):
                act.wait_ge(norm_ok, max(1, 2 * b))
                for e in range(ET):
                    act.activation(sz[:, b % 2, e, :], xs[:, b % 2, e, :], ACT.Silu, bias=nmr[:, e:e + 1],
                                   scale=rstd[:, e:e + 1]).then_inc(sz_ready, 1)

            def copy_xdbl(b):
                act.wait_ge(xproj_done, b + 1)
                wait(act, bc_stored, 16 * b)
                wait(act, dt_done, 4 * b)
                act.activation(xdbl[:], pp[0][0:DR + 2 * DS, :], ACT.Copy).then_inc(xdbl_ready, 1)

            def step_in(b, e, d):
                bank = pp[(e + 1) % 2 if d == 2 else 1]
                act.wait_ge(dt_done, e + (4 * b + 1))
                act.activation(part(delta, b, e), bank[:], ACT.Abs, bias=dtbias[:, bass.ds(e, 1)])
                act.activation(part(du, b, e), bank[:], ACT.Relu, bias=dtbias[:, bass.ds(e, 1)]).then_inc(dt_read, 1)

            def step_exp(b, lo=0, hi=ET):
                act.wait_ge(dt_read, 4 * b + hi)
                act.activation(delta[:, b % 2, lo:hi], delta[:, b % 2, lo:hi], ACT.Exp, scale=-1.0).then_inc(dt_exp, 1)

            def step_log(b, lo=0, hi=ET):
                act.wait_ge(dt_exp, 1 if hi < ET else b + 2)
                act.activation(delta[:, b % 2, lo:hi], delta[:, b % 2, lo:hi], ACT.Ln, bias=1.0).then_inc(dt_log, 1)

            def high(b, c, d):
                t = c + LC * b
                s = c % 2 if d == 2 else 0
                act.wait_ge(norm_ok, 2 * b + 3 if b < NB - 1 else 2 * NB)
                wait(act, xnT_done, t + 1 - d)
                wait(act, row_ready, t + 1 - d)
                tile = xs[:].rearrange("p b e l -> p (b e l)")[:, bass.ds(c * H + (b % 2) * (LC * H), H)]
                act.activation(xn[:, s, :], tile, ACT.Identity, scale=rstd[:, bass.ds(c, 1)],
                               bias=nmr[:, bass.ds(c, 1)]).then_inc(xn_ready, 1)
                if d == 1:
                    wait(act, row_stored[0], t * 16)
                elif c % 2 == 0:
                    act.wait_ge(row_stored[0], 16 * (LC * b + c // 2))
                else:
                    wait(act, row_stored[1], 16 * (c // 2))
                act.wait_ge(xn_ready, t + 1)
                act.activation(row[:, s, 0:H], xn[:, s, :], ACT.Copy).then_inc(hi_ready, 1)

            def copy_xnT(b, c, d):
                t = c + LC * b
                act.wait_ge(xnT_done, t + 1)
                wait(act, gate_done, t + 1 - d)
                act.activation(xnT[:, c % 2 if d == 2 else 0, :], pp[c % 2 if d == 2 else 1][:],
                               ACT.Copy).then_inc(xnT_copied, 1)

            def scan(b, e):
                act.wait_ge(delta_ready, 4 * b + e + 1)
                act.wait_ge(dve_const, 2)
                start = (4 * b + e) * DS

                def decay(q, r):
                    if start or not first(q):
                        act.wait_ge(scan_done, q * 4 + (start + r - 3))
                    act.activation(dA[r][:], delta[:, b % 2, e, :], ACT.Exp,
                                   scale=negA[:, bass.ds(q * 4 + (e * DS + r), 1)]).then_inc(dA_ready, 1)

                def four(q):
                    decay(q, 0)
                    decay(q, 1)
                    if b + 1 < NB:
                        if e == 0:
                            conv_in(b + 1, q, 1)
                        if e == 1 and q == 1:
                            copy_xdbl(b + 1)
                        if e == 3 and q == 1:
                            step_log(b + 1)
                    decay(q, 2)
                    decay(q, 3)
                    if b == 0 and e == 0 and first(q):
                        step_log(0, 1, ET)
                    if b + 1 < NB:
                        if e == 0 and last(q):
                            silu_u(b + 1)
                        if e == 2 and not first(q):
                            step_in(b + 1, q - 1, 1)
                        if e == 3 and q == 0:
                            step_in(b + 1, 3, 1)
                            step_exp(b + 1)
                        if e == 3 and q == 2:
                            silu_z(b + 1)
                    if b:
                        if e == 1:
                            if not first(q):
                                copy_xnT(b - 1, q - 1, 1)
                            high(b - 1, q, 1)
                        if e == 2 and first(q):
                            copy_xnT(b - 1, 3, 1)

                quads(act.Fori, four, straight=e in (1, 3) and b + 1 < NB)

            for e in range(ET):
                conv_in(0, e, 2)
                if e:
                    silu_first(e - 1)
            silu_first(ET - 1)
            silu_z(0)
            copy_xdbl(0)
            step_in(0, 0, 2)
            step_exp(0, 0, 1)
            step_log(0, 0, 1)
            for e in range(1, ET):
                step_in(0, e, 2)
            step_exp(0, 1, ET)
            for b in range(NB):
                for e in range(ET):
                    scan(b, e)
            def hi_up(b, k):
                if k == 0:
                    act.wait_ge(up_in[b.s], half_count(b.wn, b.s, 16))
                wait(act, up_done, b.n * NC - NC)
                act.activation(up_hl[:, b.s, 0, k, :], up_raw[:, b.s, k, :], ACT.Copy, scale=WS).then_inc(up_hi, 1)

            def hi_dn(b):
                act.wait_ge(dn_in[b.s], half_count(b.wn, b.s, 32))
                wait(act, down_done, b.t_prev)
                act.activation(dn_hl[:, b.s, 0, 0:2, :], dn_raw[:, b.s, 0:2, :], ACT.Copy, scale=WS)
                m = IC[-1][1]
                act.activation(dn_hl[0:m, b.s, 0, 2, :], dn_raw[0:m, b.s, 2, :], ACT.Copy, scale=WS).then_inc(dn_hi, 1)

            def silu(b, c):
                act.wait_ge(up_done, b.n * NC + (c + 1))
                wait(act, a_ok, b.n * NC + (c + 1 - NC))
                m = IC[c][1]
                act.activation(sg[0:m, c, 0:b.w], pu[c][0:m, 0:b.w], ACT.Silu, scale=1.0 / WS).then_inc(silu_ok, 1)

            def hi_a(b, c):
                act.wait_ge(a_ok, b.n * NC + (c + 1))
                wait(act, down_done, b.t_prev)
                m = IC[c][1]
                act.activation(a_hl[0:m, b.s, 0, c, 0:b.w], a32[0:m, c, 0:b.w], ACT.Copy).then_inc(a_hi, 1)

            def turn(cur, nxt, after):
                if nxt is None:
                    return
                split = after is not None and after.new_w
                if nxt.new_w:
                    hi_dn(nxt)
                if split:
                    hi_up(after, 0)
                for c in range(NC):
                    silu(nxt, c)
                    if split:
                        hi_up(after, c + 1)
                    hi_a(nxt, c)

            scan_over(act)
            for c in range(LC):
                hi_up(blk(0), c)
                high(NB - 1, c, 2)
                copy_xnT(NB - 1, c, 2)
            act.wait_ge(shifted, 1)
            act.activation(r_exp[:], r_exp[:], ACT.Exp).then_inc(exp_ready, 1)
            hi_dn(blk(0))
            for k in range(KT):
                hi_up(blk(1), k)
            for c in range(NC):
                silu(blk(0), c)
                hi_a(blk(0), c)
            expert_turns(turn, act.Fori)

        @block.tensor
        def _(pe):
            def in_proj(b, e, d):
                n = e + 4 * b
                if d == 2:
                    wait(pe, xin_ready, n - 1)
                elif first(e):
                    pe.wait_ge(ctx_in, 16 * (b + 1))
                    pe.wait_ge(xdbl_ready, b)
                    pe.wait_ge(dt_read, 4)
                    wait(pe, lg_copied, b - 2)
                else:
                    pe.wait_ge(xin_ready, n)
                for k in range(DM // P):
                    mm = pe.matmul(pp[e % 2 if d == 2 else 0][:], inp_w[:, k, bass.ds(e * P, P)], ctxs[:, k, :],
                                   start=(k == 0), stop=(k == DM // P - 1))
                mm.then_inc(inproj_done, 1)

            def x_proj(b, tiles):
                for e in tiles:
                    if b or e == ET - 1:
                        pe.wait_ge(u_ready, b + 1)
                    else:
                        pe.wait_ge(u_first, e + 1)
                    mm = pe.matmul(pp[0][0:DR + 2 * DS, :], xp_w[:, e, :], u[:, b % 2, e, :],
                                   start=(e == 0), stop=(e == ET - 1), skip_group_check=True)
                if e == ET - 1:
                    mm.then_inc(xproj_done, 1)

            def dt_proj(b, e, d):
                n = e + 4 * b
                pe.wait_ge(xdbl_ready, b + 1)
                wait(pe, dt_read, n + 1 - d)
                if b >= 2:
                    pe.wait_ge(xnT_copied, 4 * (b - 1))
                pe.matmul(pp[(e + 1) % 2 if d == 2 else 1][:], dt_w[:, bass.ds(e * P, P)], xdbl[0:DR, :],
                          start=True, stop=True).then_inc(dt_done, 1)

            def turn_y(b, c, d):
                t = c + LC * b
                if first(c):
                    pe.wait_ge(yv_done, 4 * b + 4)
                    pe.wait_ge(dt_read, 4 * min(b + 2, NB))
                    wait(pe, lg_copied, b)
                if d == 1:
                    wait(pe, x2_ready, t)
                elif c >= 2:
                    pe.wait_ge(x2_ready, t - 1)
                for e in range(ET):
                    mm = pe.transpose(pp[c % 2 if d == 2 else 1][:, e * P:(e + 1) * P], yv[:, e, bass.ds(c * P, P)],
                                      ident[:])
                mm.then_inc(yT_done, 1)

            def turn_xn(b, c, d):
                t = c + LC * b
                s = c % 2 if d == 2 else 0
                pe.wait_ge(xn_ready, t + 1)
                if first(c):
                    pe.wait_ge(x2_ready, LC * b + LC)
                elif d == 1 or c >= 2:
                    pe.wait_ge(xnT_copied, t + 1 - d)
                for k in range(H // P):
                    mm = pe.transpose(pp[c % 2 if d == 2 else 1][:, k * P:(k + 1) * P], xn[:, s, k * P:(k + 1) * P],
                                      ident[:])
                mm.then_inc(xnT_done, 1)

            def gate(b, c, d):
                bank = yp[1] if d == 2 else pp[0]
                pe.wait_ge(xnT_copied, c + (LC * b + 1))
                if first(c):
                    pe.wait_ge(xdbl_ready, min(b + 3, NB))
                    wait(pe, lg_copied, b)
                for k in range(H // P):
                    mm = pe.matmul(bank[:, bass.ds(c * E, E)], xnT[:, c % 2 if d == 2 else 0, k * P:(k + 1) * P],
                                   gate_w[:, k, :], start=(k == 0), stop=(k == H // P - 1), skip_group_check=True)
                mm.then_inc(gate_done, 1)

            def scan(b, e):
                n = 4 * b + e
                start = n * DS
                if n:
                    wait(pe, yv_done, n - 1)
                else:
                    pe.wait_ge(dve_const, 3)
                pe.matmul(yp[n % 2][:], Ddiag[:, e, :], u[:, b % 2, e, :], start=True, stop=False,
                          skip_group_check=True)
                if n == 0:
                    in_proj(1, 0, 1)

                def add(q, r):
                    pe.wait_ge(hc_ready, q * 4 + (start + r + 1))
                    pe.matmul(yp[n % 2][:], ident[:], hc[:, r, :], start=False, stop=False,
                              skip_group_check=True).then_inc(sum_done, 1)

                def four(q):
                    add(q, 0)
                    add(q, 1)
                    if e == 0:
                        if b:
                            turn_y(b - 1, q, 1)
                        if b + 1 < NB and not last(q):
                            in_proj(b + 1, q + 1, 1)
                    if e == 1 and b + 1 < NB and first(q):
                        x_proj(b + 1, range(0, 2))
                    add(q, 2)
                    add(q, 3)
                    if e == 1 and b + 1 < NB and first(q):
                        x_proj(b + 1, range(2, 4))
                    if e == 1 and b:
                        if not first(q):
                            gate(b - 1, q - 1, 1)
                        turn_xn(b - 1, q, 1)
                    if e == 3 and b + 2 < NB and q == 2:
                        in_proj(b + 2, 0, 1)
                    if e == 2:
                        if b and first(q):
                            gate(b - 1, 3, 1)
                        if b + 1 < NB:
                            dt_proj(b + 1, q, 1)

                quads(pe.Fori, four, straight=e < 3 or b + 2 < NB)

            pe.wait_ge(ident_ok, 1)
            pe.wait_ge(inp_in, 16)
            pe.wait_ge(ctx_in, 16)
            for e in range(ET):
                in_proj(0, e, 2)
            pe.wait_ge(w_in, 16 * 8)
            pe.wait_ge(xin_ready, ET - 1)
            x_proj(0, range(ET))
            for e in range(ET):
                dt_proj(0, e, 2)
            for b in range(NB):
                for e in range(ET):
                    scan(b, e)
            for c in range(LC):
                turn_y(NB - 1, c, 2)
            for c in range(LC):
                turn_xn(NB - 1, c, 2)
                if c:
                    gate(NB - 1, c - 1, 2)
            gate(NB - 1, LC - 1, 2)

            def up(b):
                pe.wait_ge(up_lo, b.wn * KT + KT)
                pe.wait_ge(xT_in[b.s], half_count(b.n, b.s, 16))
                for c, (at, m) in enumerate(IC):
                    wait(pe, a_ok, b.n * NC + (c + 1 - NC))
                    for half in range(2):
                        steps = [(w, v, k) for w, v in ((0, 0), (1, 0), (0, 1)) for k in range(KT)]
                        for j, (w, v, k) in enumerate(steps):
                            mm = pe.matmul(pu[c][0:m, half * TB:half * TB + b.w],
                                           up_hl[:, b.s, w, k, half * I + at:half * I + at + m],
                                           xT[:, b.s, v * KT + k, 0:b.w], start=(j == 0), stop=(j == len(steps) - 1))
                    mm.then_inc(up_done, 1)

            def down(b):
                pe.wait_ge(dn_lo, b.wn + 1)
                pe.wait_ge(a_lo, b.n * NC + NC)
                for t in range(b.bt):
                    wait(pe, y_ok, b.t_prev + min(t + 1, b.bt_prev))
                    steps = [(c, w, v) for c in range(NC) for w, v in ((0, 0), (1, 0), (0, 1))]
                    for j, (c, w, v) in enumerate(steps):
                        m = IC[c][1]
                        mm = pe.matmul(py[t][:], a_hl[0:m, b.s, v, c, t * P:(t + 1) * P], dn_hl[0:m, b.s, w, c, :],
                                       start=(j == 0), stop=(j == len(steps) - 1))
                    mm.then_inc(down_done, 1)

            def turn(cur, nxt, after):
                if nxt:
                    up(nxt)
                down(cur)

            scan_over(pe)
            up(blk(0))

            def turn_and_rank(cur, nxt, after):
                turn(cur, nxt, after)
                if cur is not None and isinstance(cur.n, int) and cur.n == RANK_AT:
                    pe.wait_ge(mask_ready, 1)
                    pe.wait_ge(route_const, 8)
                    flat = picked[:].rearrange("p t e -> p (t e)")
                    pe.matmul(pr[:, 0:NT * E], before[:], flat, start=True, stop=True)
                    pe.matmul(pr[:, NT * E:], ones[:], flat, start=True, stop=True).then_inc(rank_done, 1)

            expert_turns(turn_and_rank, pe.Fori)

        @block.vector
        def _(dve):
            steps = [0]

            def link(ins):
                steps[0] += 1
                ins.then_inc(chain, 1)
                dve.wait_ge(chain, steps[0])

            dve.memset(wshared[:], 1.0 / WS)
            dve.memset(xin[:, :, 0:TAPS - 1], 0.0).then_inc(dve_const, 1)
            dve.wait_ge(act_const, 1)
            dve.tensor_scalar(negA[:], alog[:], -1.0, None, ALU.mult).then_inc(dve_const, 1)
            dve.wait_ge(ident_ok, 1)
            for e in range(ET):
                ins = dve.tensor_scalar(Ddiag[:, e, :], ident[:], Dcol[:, e:e + 1], None, ALU.mult)
            ins.then_inc(dve_const, 1)
            dve.wait_ge(dve_const, 3)

            def moments(b):
                for c in range(LC):
                    ins = dve.bn_stats(stat[:, c, :], xs[:, b % 2, c, :])
                link(ins)
                for c in range(LC):
                    ins = dve.bn_aggr(mv[:, c, :], stat[:, c, :])
                link(ins)
                dve.tensor_scalar(veps[:], mv[:, :, 1], EPS, None, ALU.add).then_inc(ln_var, 1)

            def norm_scale(n):
                dve.wait_ge(ln_rstd, n + 1)
                dve.scalar_tensor_tensor(out=nmr[:], in0=mv[:, :, 0], scalar=-1.0, in1=rstd[:],
                                         op0=ALU.mult, op1=ALU.mult).then_inc(norm_ok, 1)

            def conv(b, e, d):
                n = e + 4 * b
                s = e % 2 if d == 2 else 0
                dve.wait_ge(xin_ready, n + 1)
                for k in range(TAPS - 1):
                    ins = dve.scalar_tensor_tensor(out=part(u, b, e), in0=xin[:, s, k:k + L],
                                                   scalar=taps[:, bass.ds(e * TAPS + k, 1)], in1=part(u, b, e),
                                                   op0=ALU.mult, op1=ALU.add)
                    if k < TAPS - 2:
                        ins.then_inc(conv_tap, 1)
                        dve.wait_ge(conv_tap, n * (TAPS - 2) + (k + 1))
                ins.then_inc(conv_done, 1)

            def xtile(b, c):
                return xs[:].rearrange("p b e l -> p (b e l)")[:, bass.ds(c * H + (b % 2) * (LC * H), H)]

            def gated(n):
                b, e = divmod(n, ET)
                dve.wait_ge(sum_done, DS * (n + 1))
                dve.wait_ge(sz_ready, n + 1)
                dve.tensor_tensor(yv[:, e, :], yp[n % 2][:], sz[:, b % 2, e, :], ALU.mult).then_inc(yv_done, 1)

            def add_x(b, c, d):
                dve.wait_ge(yT_done, c + (LC * b + 1))
                dve.tensor_tensor(xtile(b, c), pp[c % 2 if d == 2 else 1][:], xtile(b, c),
                                  ALU.add).then_inc(x2_ready, 1)

            def low(b, c, d):
                t = c + LC * b
                s = c % 2 if d == 2 else 0
                dve.wait_ge(xn_ready, t + 1)
                dve.wait_ge(hi_ready, t + 1)
                dve.tensor_copy(row[:, s, RW - 2:RW].bitcast(I32), tokens[:, bass.ds(t, 1)])
                dve.tensor_copy(row[:, s, RW - 4:RW - 2].bitcast(F32), wshared[:])
                dve.tensor_tensor(row[:, s, H:2 * H], xn[:, s, :], row[:, s, 0:H], ALU.subtract).then_inc(row_ready, 1)

            def keep_logits(b, bank):
                dve.wait_ge(gate_done, LC * b + LC)
                dve.tensor_copy(logits[:, LC * b:LC * b + LC, :],
                                bank[:, 0:LC * E].rearrange("p (t e) -> p t e", e=E)).then_inc(lg_copied, 1)

            def scan(b, e):
                n = 4 * b + e
                start = n * DS

                def recur(q, r, free=True):
                    dve.wait_ge(dA_ready, q * 4 + (start + r + 1))
                    if r % 2 == 0:
                        dve.wait_ge(dbu_ready, q * 2 + (start // 2 + r // 2 + 1))
                    if free:
                        dve.wait_ge(sum_done, q * 4 + (start + r - 3))
                    dve.tensor_tensor_scan(hc[:, r % 4, :], dA[r][:], dBu[:, (r // 2) % 2, r % 2, :], 0.0,
                                           ALU.mult, ALU.add).then_inc(scan_done, 1)

                def weigh(q, r):
                    dve.wait_ge(scan_done, q * 4 + (start + r + 1))
                    dve.tensor_tensor(hc[:, r, :], hc[:, r, :], Cf[:, bass.ds(q * (4 * L) + r * L, L)],
                                      ALU.mult).then_inc(hc_ready, 1)

                def four(q):
                    if e == 0:
                        dve.wait_ge(c_ready, q * 16 + 16 * (4 * b + 1))
                    for r in range(4):
                        if r < 3:
                            recur(q, r + 1, free=start or not first(q))
                        elif not last(q):
                            recur(q + 1, 0)
                        weigh(q, r)
                        if r == 1:
                            between(q)
                    after(q)

                def between(q):
                    if n and first(q):
                        gated(n - 1)
                    if b + 1 < NB:
                        if e == 0:
                            conv(b + 1, q, 1)
                        if e == 3:
                            if first(q):
                                norm_scale(2 * b + 1)
                    if b and e == 1 and first(q):
                        norm_scale(2 * b)

                def after(q):
                    if b + 1 < NB:
                        if e == 2 and last(q):
                            dve.wait_ge(x_in, 16 * (b + 2))
                            moments(b + 1)
                    if b:
                        if e == 0:
                            add_x(b - 1, q, 1)
                            if last(q):
                                dve.wait_ge(x2_ready, LC * b)
                                moments(b - 1)
                        if e == 1:
                            low(b - 1, q, 1)
                        if e == 2 and last(q):
                            keep_logits(b - 1, pp[0])

                recur(0, 0, free=start > 0)
                quads(dve.Fori, four)

            conv(0, 0, 2)
            conv(0, 1, 2)
            dve.wait_ge(x_in, 16)
            moments(0)
            conv(0, 2, 2)
            conv(0, 3, 2)
            norm_scale(0)
            for b in range(NB):
                for e in range(ET):
                    scan(b, e)
            def lo_up(b, k):
                dve.wait_ge(up_hi, b.wn * KT + (k + 1))
                wait(dve, up_done, b.n * NC - NC)
                dve.scalar_tensor_tensor(out=up_hl[:, b.s, 1, k, :], in0=up_raw[:, b.s, k, :], scalar=WS,
                                         in1=up_hl[:, b.s, 0, k, :], op0=ALU.mult,
                                         op1=ALU.subtract).then_inc(up_lo, 1)

            def lo_dn(b):
                dve.wait_ge(dn_hi, b.wn + 1)
                m = IC[-1][1]
                dve.scalar_tensor_tensor(out=dn_hl[:, b.s, 1, 0:2, :], in0=dn_raw[:, b.s, 0:2, :], scalar=WS,
                                         in1=dn_hl[:, b.s, 0, 0:2, :], op0=ALU.mult, op1=ALU.subtract)
                dve.scalar_tensor_tensor(out=dn_hl[0:m, b.s, 1, 2, :], in0=dn_raw[0:m, b.s, 2, :], scalar=WS,
                                         in1=dn_hl[0:m, b.s, 0, 2, :], op0=ALU.mult,
                                         op1=ALU.subtract).then_inc(dn_lo, 1)

            def gate_up(b, c):
                dve.wait_ge(silu_ok, b.n * NC + (c + 1))
                wait(dve, a_lo, b.n * NC + (c + 1 - NC))
                m = IC[c][1]
                dve.scalar_tensor_tensor(out=a32[0:m, c, 0:b.w], in0=pu[c][0:m, TB:TB + b.w], scalar=1.0 / WS,
                                         in1=sg[0:m, c, 0:b.w], op0=ALU.mult, op1=ALU.mult).then_inc(a_ok, 1)

            def lo_a(b, c):
                dve.wait_ge(a_hi, b.n * NC + (c + 1))
                m = IC[c][1]
                dve.tensor_tensor(a_hl[0:m, b.s, 1, c, 0:b.w], a32[0:m, c, 0:b.w], a_hl[0:m, b.s, 0, c, 0:b.w],
                                  ALU.subtract).then_inc(a_lo, 1)

            def weigh_y(b):
                wait(dve, y_added, b.t_prev * 16)
                dve.tensor_copy(dest[:, b.s, 0:b.bt], meta[:, bass.ds(b.m, b.bt), 1])
                for t in range(b.bt):
                    dve.wait_ge(down_done, b.t + (t + 1))
                    dve.tensor_scalar(yb[:, b.s, t, :], py[t][:], meta[:, bass.ds(b.m + t, 1), 0].bitcast(F32),
                                      None, ALU.mult).then_inc(y_ok, 1)

            def turn(cur, nxt, after):
                if nxt:
                    split = after is not None and after.new_w
                    if nxt.new_w:
                        lo_dn(nxt)
                    if split:
                        lo_up(after, 0)
                    for c in range(NC):
                        gate_up(nxt, c)
                        if split:
                            lo_up(after, c + 1)
                        lo_a(nxt, c)
                weigh_y(cur)

            gated(4 * NB - 1)
            for c in range(LC):
                add_x(NB - 1, c, 2)
            dve.wait_ge(x2_ready, NT)
            moments(NB - 1)
            norm_scale(2 * NB - 1)
            for c in range(LC):
                low(NB - 1, c, 2)
                lo_up(blk(0), c)
            keep_logits(NB - 1, yp[1])

            def rows3(ap, n):
                return ap.unsqueeze(2).to_broadcast([P, ap.shape[1], n])

            def cols3(ap, n):
                return ap.unsqueeze(1).to_broadcast([P, n, ap.shape[1]])

            dve.wait_ge(lg_copied, NB)
            link(dve.tensor_reduce(r_max[:], logits[:], AX.X, ALU.max))
            dve.tensor_tensor(r_exp[:], logits[:], rows3(r_max[:], E), ALU.subtract).then_inc(shifted, 1)
            dve.memset(g_in[:], -1.0)

            def route_0():
                dve.wait_ge(exp_ready, 1)
                link(dve.tensor_reduce(r_sum[:], r_exp[:], AX.X, ALU.add))
                link(dve.reciprocal(r_inv[:], r_sum[:]))
                link(dve.tensor_tensor(score[:], r_exp[:], rows3(r_inv[:], E), ALU.mult))
                link(dve.tensor_reduce(g_in[:, :, 0:G], score[:].rearrange("p t (g j) -> p t g j", g=G), AX.X, ALU.max))
                for t in range(NT):
                    ins = dve.max(g_top[:, t, :], g_in[:, t, :])
                link(ins)
                for t in range(NT):
                    ins = dve.max_index(g_idx[:, t, :], g_top[:, t, :], g_in[:, t, :])
                link(ins)

            def route_1():
                dve.wait_ge(route_const, 8)
                link(dve.tensor_copy(g_idf[:], g_idx[:]))
                dve.tensor_tensor(g_mask[:], cols3(iota_e[:, 0:G], NT), g_idf[:, :, 0:1].to_broadcast([P, NT, G]),
                                  ALU.is_equal)
                link(dve.tensor_tensor(g_mask2[:], cols3(iota_e[:, 0:G], NT), g_idf[:, :, 1:2].to_broadcast([P, NT, G]),
                                       ALU.is_equal))
                link(dve.tensor_tensor(g_mask[:], g_mask[:], g_mask2[:], ALU.add))
                link(dve.tensor_tensor(score[:].rearrange("p t (g j) -> p (t g) j", g=G),
                                       score[:].rearrange("p t (g j) -> p (t g) j", g=G),
                                       rows3(g_mask[:].rearrange("p t g -> p (t g)"), E // G), ALU.mult))
                for t in range(NT):
                    ins = dve.max(e_top[:, t, :], score[:, t, :])
                link(ins)
                for t in range(NT):
                    ins = dve.max_index(e_idx[:, t, :], e_top[:, t, :], score[:, t, :])
                link(ins)
                link(dve.tensor_copy(e_idf[:], e_idx[:]))

            def route_2():
                for k in range(TOPK):
                    ins = dve.tensor_tensor(onehot[:, k], cols3(iota_e[:], NT),
                                            e_idf[:, :, k:k + 1].to_broadcast([P, NT, E]), ALU.is_equal)
                link(ins)
                link(dve.tensor_tensor(picked[:], onehot[:, 0], onehot[:, 1], ALU.add))
                link(dve.tensor_tensor(picked[:], picked[:], onehot[:, 2], ALU.add))
                dve.tensor_tensor(picked[:], picked[:], onehot[:, 3], ALU.add).then_inc(mask_ready, 1)
                link(dve.tensor_reduce(r_sum[:], e_top[:, :, 0:TOPK], AX.X, ALU.add))
                link(dve.tensor_scalar(r_sum[:], r_sum[:], 1e-20, None, ALU.add))
                link(dve.reciprocal(r_inv[:], r_sum[:]))
                link(dve.tensor_tensor(w_top[:], e_top[:, :, 0:TOPK], rows3(r_inv[:], TOPK), ALU.mult))
                link(dve.tensor_scalar(w_top[:], w_top[:], 1.0 / WS, None, ALU.mult))

            def route_3():
                dve.wait_ge(rank_done, 1)
                link(dve.tensor_copy(count[:], pr[:, NT * E:].rearrange("p (t e) -> p e t", e=E)))
                flat = lambda a: a[:].rearrange("p e t -> p (e t)")
                link(dve.tensor_tensor_scan(flat(cum_t), flat(keep), flat(count), 0.0, ALU.mult, ALU.add))
                link(dve.tensor_tensor(over[:], cum_t[:, :, NT - 1:NT].to_broadcast([P, E, NT]), cols3(iota_m[:], E),
                                       ALU.is_gt))
                dve.tensor_reduce(big_e[:], over[:].rearrange("p e (m two) -> p e m two", two=2)[:, :, :, 1], AX.X, ALU.add)
                link(dve.tensor_reduce(tiles_e[:], over[:], AX.X, ALU.add))
                link(dve.tensor_tensor_scan(big_to[:], ones[:, 0:E], big_e[:], 0.0, ALU.mult, ALU.add))
                link(dve.tensor_tensor(big_from[:], big_to[:], big_e[:], ALU.subtract))
                dve.tensor_scalar(big_to[:], big_to[:], float(NBIG), None, ALU.min)
                link(dve.tensor_scalar(big_from[:], big_from[:], float(NBIG), None, ALU.min))
                link(dve.tensor_tensor(big_e[:], big_to[:], big_from[:], ALU.subtract))
                link(dve.scalar_tensor_tensor(out=small_e[:], in0=big_e[:], scalar=-2.0, in1=tiles_e[:],
                                              op0=ALU.mult, op1=ALU.add))
                link(dve.tensor_tensor_scan(small_to[:], ones[:, 0:E], small_e[:], 0.0, ALU.mult, ALU.add))
                dve.tensor_tensor(below[:, 0:NBIG], cols3(big_to[:], NBIG), rows3(iota_b[:, 0:NBIG], E), ALU.is_le)
                link(dve.tensor_tensor(below[:, NBIG:], cols3(small_to[:], NSMALL), rows3(iota_b[:, 0:NSMALL], E), ALU.is_le))
                link(dve.tensor_reduce(bexpf[:], below[:], AX.X, ALU.add))
                dve.tensor_scalar(bexp[:], bexpf[:], float(E - 1), None, ALU.min).then_inc(experts_ready, 1)
                dve.tensor_scalar(in_big[:], big_e[:], float(TB), None, ALU.mult)
                dve.tensor_scalar(big_from[:], big_from[:], float(TB), None, ALU.mult)
                link(dve.tensor_tensor(small_to[:], small_to[:], small_e[:], ALU.subtract))
                link(dve.tensor_scalar(to_small[:], small_to[:], float(P), float(NBIG * TB), ALU.mult, ALU.add))
                link(dve.tensor_tensor(to_small[:], to_small[:], in_big[:], ALU.subtract))
                link(dve.tensor_tensor(to_small[:], to_small[:], big_from[:], ALU.subtract))

            def route_4():
                link(dve.tensor_tensor(cum_t[:], cum_t[:], count[:], ALU.subtract))
                dve.tensor_tensor(rank[:], pr[:, 0:NT * E].rearrange("p (t e) -> p t e", e=E),
                                  cum_t[:].rearrange("p e t -> p t e"), ALU.add).then_inc(rank_read, 1)
                dve.wait_ge(rank_read, 1)
                link(dve.tensor_tensor(place[:], rank[:], cols3(in_big[:], NT), ALU.is_ge))
                link(dve.tensor_tensor(place[:], place[:], cols3(to_small[:], NT), ALU.mult))
                link(dve.tensor_tensor(place[:], place[:], rank[:], ALU.add))
                link(dve.tensor_tensor(place[:], place[:], cols3(big_from[:], NT), ALU.add))
                for k in range(TOPK):
                    link(dve.tensor_tensor(prod[:], onehot[:, k], place[:], ALU.mult))
                    link(dve.tensor_reduce(slotf[:, k, :], prod[:], AX.X, ALU.add))
                dve.tensor_copy(slot[:], slotf[:]).then_inc(slot_ok, 1)

            routing = (route_0, route_1, route_2, route_3, route_4)

            def turn_and_route(cur, nxt, after):
                if cur is not None and isinstance(cur.n, int) and cur.n < len(routing):
                    routing[cur.n]()
                turn(cur, nxt, after)

            lo_dn(blk(0))
            for k in range(KT):
                lo_up(blk(1), k)
            for c in range(NC):
                gate_up(blk(0), c)
                lo_a(blk(0), c)
            dve.wait_ge(meta_ok, 2)
            expert_turns(turn_and_route, dve.Fori, before_routed=lambda: dve.wait_ge(meta_in, 16))

def kernel(**inputs):
    import numpy as np
    import concourse.bacc as bacc
    from concourse.bass_utils import run_bass_kernel_spmd

    def tiles(a):
        return np.ascontiguousarray(a.reshape((-1, 128) + a.shape[1:]).swapaxes(0, 1))

    up = np.concatenate([inputs["L0_ffn_expert_up_w"],
                         inputs["L0_ffn_shared_up_w"].reshape(2, 2, 352, 512).swapaxes(0, 1).reshape(2, 704, 512)])
    down = np.concatenate([inputs["L0_ffn_expert_down_w"],
                           inputs["L0_ffn_shared_down_w"].reshape(512, 2, 352).swapaxes(0, 1)])
    upT = up.transpose(0, 2, 1).reshape(18, 4, 128, 704).transpose(0, 2, 1, 3)
    downT = down.transpose(0, 2, 1)
    arrays = {
        "x": inputs["x"].reshape(4, 4, 128, 512).transpose(0, 2, 1, 3),
        "ctxT": inputs["ctx_1024"].transpose(0, 2, 1).reshape(4, 2, 128, 512).transpose(0, 2, 1, 3),
        "in_projT": tiles(inputs["L0_xattn_in_proj_w"].T),
        "conv_w": tiles(inputs["L0_xattn_conv_w"]).reshape(128, 16),
        "conv_b": tiles(inputs["L0_xattn_conv_b"]),
        "x_projT": tiles(inputs["L0_xattn_x_proj_w"].T),
        "dt_projT": inputs["L0_xattn_dt_proj_w"].T,
        "dt_b": tiles(inputs["L0_xattn_dt_proj_b"]),
        "A_log": tiles(inputs["L0_xattn_A_log"]).reshape(128, 64),
        "D": tiles(inputs["L0_xattn_D"]),
        "gateT": tiles(inputs["L0_ffn_gate_w"].T),
        "upT": upT,
        "downA": downT[:, :256].reshape(18, 2, 128, 512).transpose(0, 2, 1, 3),
        "downB": downT[:, 256:],
    }
    nc = bacc.Bacc("TRN2", target_bir_lowering=False, num_devices=1)
    feed, args = {}, []
    for name, a in arrays.items():
        a = np.ascontiguousarray(a)
        feed[f"in_{name}"] = a
        args.append(nc.dram_tensor(f"in_{name}", a.shape, mybir.dt.from_np(a.dtype), kind="ExternalInput").ap())
    args.append(nc.dram_tensor("out_0", (2048 + 256, 512), F32, kind="ExternalOutput").ap())
    build(nc, *args)
    got = run_bass_kernel_spmd(nc, [feed], core_ids=[0])
    return got.results[0]["out_0"][:2048].reshape(4, 512, 512)
```
